# Optimizing a Trainium2 kernel written in Bass

```python
import numpy as np
import jax
import jax.numpy as jnp

def _softmax(x, axis=-1):
    return jax.nn.softmax(x, axis=axis)

def _gelu(x):
    return jax.nn.gelu(x, approximate=True)

def _silu(x):
    return jax.nn.silu(x)

def _sigmoid(x):
    return jax.nn.sigmoid(x)

def _layernorm(x, axis=-1, eps=1e-05):
    m = jnp.mean(x, axis=axis, keepdims=True)
    v = jnp.var(x, axis=axis, keepdims=True)
    return (x - m) / jnp.sqrt(v + eps)

def _scatter_add(tgt, idx, src, axis=0):
    return tgt.at[idx].add(src)

def _segment_sum(src, seg, n):
    return jax.ops.segment_sum(src, seg, n)
kernel_name = 'mk_dlrm_tower_d1_rec_r8_6d1f04'

def setup_inputs(seed: int=0):
    np.random.seed(seed)
    _w = jnp.asarray

    def _rec_inputs():
        import jax
        import jax.numpy as jnp
        _tk = jax.random.key(seed)
        ids = jnp.stack([jax.random.randint(jax.random.fold_in(_tk, 200 + f), (2048,), 0, v, jnp.int32) for f, v in enumerate([1250, 125000, 1000, 1250, 12500, 1000, 1000, 12500, 12500, 1250, 1000, 1250, 12500, 1000, 1000, 12500, 1250, 12500, 1250, 12500, 1000, 1250, 1000, 1000, 1000, 1250])], axis=1)
        tbl_0 = 0.05 * jax.random.normal(jax.random.fold_in(_tk, 500 + 0), (1250, 128), jnp.float32)
        tbl_1 = 0.05 * jax.random.normal(jax.random.fold_in(_tk, 500 + 1), (125000, 128), jnp.float32)
        tbl_2 = 0.05 * jax.random.normal(jax.random.fold_in(_tk, 500 + 2), (1000, 128), jnp.float32)
        tbl_3 = 0.05 * jax.random.normal(jax.random.fold_in(_tk, 500 + 3), (1250, 128), jnp.float32)
        tbl_4 = 0.05 * jax.random.normal(jax.random.fold_in(_tk, 500 + 4), (12500, 128), jnp.float32)
        tbl_5 = 0.05 * jax.random.normal(jax.random.fold_in(_tk, 500 + 5), (1000, 128), jnp.float32)
        tbl_6 = 0.05 * jax.random.normal(jax.random.fold_in(_tk, 500 + 6), (1000, 128), jnp.float32)
        tbl_7 = 0.05 * jax.random.normal(jax.random.fold_in(_tk, 500 + 7), (12500, 128), jnp.float32)
        tbl_8 = 0.05 * jax.random.normal(jax.random.fold_in(_tk, 500 + 8), (12500, 128), jnp.float32)
        tbl_9 = 0.05 * jax.random.normal(jax.random.fold_in(_tk, 500 + 9), (1250, 128), jnp.float32)
        tbl_10 = 0.05 * jax.random.normal(jax.random.fold_in(_tk, 500 + 10), (1000, 128), jnp.float32)
        tbl_11 = 0.05 * jax.random.normal(jax.random.fold_in(_tk, 500 + 11), (1250, 128), jnp.float32)
        tbl_12 = 0.05 * jax.random.normal(jax.random.fold_in(_tk, 500 + 12), (12500, 128), jnp.float32)
        tbl_13 = 0.05 * jax.random.normal(jax.random.fold_in(_tk, 500 + 13), (1000, 128), jnp.float32)
        tbl_14 = 0.05 * jax.random.normal(jax.random.fold_in(_tk, 500 + 14), (1000, 128), jnp.float32)
        tbl_15 = 0.05 * jax.random.normal(jax.random.fold_in(_tk, 500 + 15), (12500, 128), jnp.float32)
        tbl_16 = 0.05 * jax.random.normal(jax.random.fold_in(_tk, 500 + 16), (1250, 128), jnp.float32)
        tbl_17 = 0.05 * jax.random.normal(jax.random.fold_in(_tk, 500 + 17), (12500, 128), jnp.float32)
        tbl_18 = 0.05 * jax.random.normal(jax.random.fold_in(_tk, 500 + 18), (1250, 128), jnp.float32)
        tbl_19 = 0.05 * jax.random.normal(jax.random.fold_in(_tk, 500 + 19), (12500, 128), jnp.float32)
        tbl_20 = 0.05 * jax.random.normal(jax.random.fold_in(_tk, 500 + 20), (1000, 128), jnp.float32)
        tbl_21 = 0.05 * jax.random.normal(jax.random.fold_in(_tk, 500 + 21), (1250, 128), jnp.float32)
        tbl_22 = 0.05 * jax.random.normal(jax.random.fold_in(_tk, 500 + 22), (1000, 128), jnp.float32)
        tbl_23 = 0.05 * jax.random.normal(jax.random.fold_in(_tk, 500 + 23), (1000, 128), jnp.float32)
        tbl_24 = 0.05 * jax.random.normal(jax.random.fold_in(_tk, 500 + 24), (1000, 128), jnp.float32)
        tbl_25 = 0.05 * jax.random.normal(jax.random.fold_in(_tk, 500 + 25), (1250, 128), jnp.float32)
        _rk = jax.random.fold_in(_tk, 7)
        r_dense_features = -0.000520686 + 1.00062 * jax.random.normal(jax.random.fold_in(_rk, 101), (2048, 128), jnp.float32)
        W_top1 = 0.0405887 * jax.random.normal(jax.random.fold_in(_tk, 801), (607, 512), jnp.float32)
        W_top2 = 0.0441942 * jax.random.normal(jax.random.fold_in(_tk, 802), (512, 256), jnp.float32)
        W_top3 = 0.0625 * jax.random.normal(jax.random.fold_in(_tk, 803), (256, 1), jnp.float32)
        b_top1 = jnp.zeros((512,), jnp.float32)
        b_top2 = jnp.zeros((256,), jnp.float32)
        return (r_dense_features, ids, tbl_0, tbl_1, tbl_2, tbl_3, tbl_4, tbl_5, tbl_6, tbl_7, tbl_8, tbl_9, tbl_10, tbl_11, tbl_12, tbl_13, tbl_14, tbl_15, tbl_16, tbl_17, tbl_18, tbl_19, tbl_20, tbl_21, tbl_22, tbl_23, tbl_24, tbl_25, W_top1, b_top1, W_top2, b_top2, W_top3)
    r_dense_features, ids, tbl_0, tbl_1, tbl_2, tbl_3, tbl_4, tbl_5, tbl_6, tbl_7, tbl_8, tbl_9, tbl_10, tbl_11, tbl_12, tbl_13, tbl_14, tbl_15, tbl_16, tbl_17, tbl_18, tbl_19, tbl_20, tbl_21, tbl_22, tbl_23, tbl_24, tbl_25, W_top1, b_top1, W_top2, b_top2, W_top3 = _rec_inputs()

    def _L0_rec_setup():
        import jax, jax.numpy as jnp
        import numpy as np
        F = 26
        B, D = (2048, 128)
        _IU0, _IU1 = np.triu_indices(F + 1, k=1)
        _IU0 = jnp.asarray(_IU0)
        _IU1 = jnp.asarray(_IU1)
        key = jax.random.key(seed)
        k1, k2 = jax.random.split(key)
        dense_features = jax.random.normal(k1, (B, D), dtype=jnp.float32)
        sparse_features = jax.random.normal(k2, (B, F, D), dtype=jnp.float32)
        return {'dense_features': dense_features, 'sparse_features': sparse_features}
    _L0_rec_all = _L0_rec_setup()
    _L0_rec_in = {k: v for k, v in _L0_rec_all.items() if k in ()}
    del _L0_rec_all
    return {'r_dense_features': r_dense_features, 'ids': ids, 'tbl_0': tbl_0, 'tbl_1': tbl_1, 'tbl_2': tbl_2, 'tbl_3': tbl_3, 'tbl_4': tbl_4, 'tbl_5': tbl_5, 'tbl_6': tbl_6, 'tbl_7': tbl_7, 'tbl_8': tbl_8, 'tbl_9': tbl_9, 'tbl_10': tbl_10, 'tbl_11': tbl_11, 'tbl_12': tbl_12, 'tbl_13': tbl_13, 'tbl_14': tbl_14, 'tbl_15': tbl_15, 'tbl_16': tbl_16, 'tbl_17': tbl_17, 'tbl_18': tbl_18, 'tbl_19': tbl_19, 'tbl_20': tbl_20, 'tbl_21': tbl_21, 'tbl_22': tbl_22, 'tbl_23': tbl_23, 'tbl_24': tbl_24, 'tbl_25': tbl_25, 'W_top1': W_top1, 'b_top1': b_top1, 'W_top2': W_top2, 'b_top2': b_top2, 'W_top3': W_top3}

def reference(r_dense_features, ids, tbl_0, tbl_1, tbl_2, tbl_3, tbl_4, tbl_5, tbl_6, tbl_7, tbl_8, tbl_9, tbl_10, tbl_11, tbl_12, tbl_13, tbl_14, tbl_15, tbl_16, tbl_17, tbl_18, tbl_19, tbl_20, tbl_21, tbl_22, tbl_23, tbl_24, tbl_25, W_top1, b_top1, W_top2, b_top2, W_top3):
    import jax
    import jax.numpy as jnp

    def _L0_rec_ref(dense_features, sparse_features):
        import jax, jax.numpy as jnp
        import numpy as np
        F = 26
        B, D = (2048, 128)
        _IU0, _IU1 = np.triu_indices(F + 1, k=1)
        _IU0 = jnp.asarray(_IU0)
        _IU1 = jnp.asarray(_IU1)
        combined = jnp.concatenate([dense_features[:, None, :], sparse_features], axis=1)
        interactions = jnp.einsum('bfd,bgd->bfg', combined, combined)
        interactions_flat = interactions[:, _IU0, _IU1]
        return jnp.concatenate([dense_features, interactions_flat], axis=1)
    e = jnp.stack([tbl_0[ids[:, 0]], tbl_1[ids[:, 1]], tbl_2[ids[:, 2]], tbl_3[ids[:, 3]], tbl_4[ids[:, 4]], tbl_5[ids[:, 5]], tbl_6[ids[:, 6]], tbl_7[ids[:, 7]], tbl_8[ids[:, 8]], tbl_9[ids[:, 9]], tbl_10[ids[:, 10]], tbl_11[ids[:, 11]], tbl_12[ids[:, 12]], tbl_13[ids[:, 13]], tbl_14[ids[:, 14]], tbl_15[ids[:, 15]], tbl_16[ids[:, 16]], tbl_17[ids[:, 17]], tbl_18[ids[:, 18]], tbl_19[ids[:, 19]], tbl_20[ids[:, 20]], tbl_21[ids[:, 21]], tbl_22[ids[:, 22]], tbl_23[ids[:, 23]], tbl_24[ids[:, 24]], tbl_25[ids[:, 25]]], axis=1)
    z = _L0_rec_ref(r_dense_features, e)
    z = z.reshape(z.shape[0], -1)
    h = jnp.concatenate([z, r_dense_features], axis=1)
    h = jnp.maximum(h @ W_top1 + b_top1, 0.0)
    h = jnp.maximum(h @ W_top2 + b_top2, 0.0)
    y = h @ W_top3
    return y

_drawn_inputs = setup_inputs


def setup_inputs(seed=0):
    import zlib

    import numpy as np

    out = dict(_drawn_inputs(seed))
    spreads = {'b_top1': (0.0, 0.1), 'b_top2': (0.0, 0.1)}
    factors = {}
    for name, (base, spread) in spreads.items():
        noise = np.random.default_rng([zlib.crc32(name.encode()), seed]).standard_normal(out[name].shape)
        drawn = base * np.exp(spread * noise) if base else spread * noise
        out[name] = jnp.asarray(drawn.astype(out[name].dtype))
    for name, factor in factors.items():
        out[name] = (out[name] * factor).astype(out[name].dtype)
    return out
```

```python
from contextlib import ExitStack

import concourse.bass as bass
from concourse import mybir

ALU = mybir.AluOpType
ACT = mybir.ActivationFunctionType
F32 = mybir.dt.float32
I32 = mybir.dt.int32
U32 = mybir.dt.uint32

P = 128
BATCH = 2048
DIM = 128
TABLES = 26
FEATS = TABLES + 1
FEATS_PAD = 32
LEFT = FEATS - 1
PAIRS = FEATS * (FEATS - 1) // 2
H1, H2 = 512, 256

TILES = BATCH // P
GTILES = 4
GROUPS = TILES // GTILES
GCOLS = GTILES * P
LANES = 4
QT = P // LANES
QH = QT // 2
HALF_GRAMS = QH * LANES

TB = 4
FEAT_BATCHES = -(-FEATS // TB)
LEFT_BATCHES = -(-LEFT // TB)
PCHUNKS = 3
PK = PAIRS // PCHUNKS
TURN_BATCHES = LEFT_BATCHES + PCHUNKS
MLP_STEPS = H1 // P + H2 // P + 1
BATCHES_EARLY = 4

assert PK * PCHUNKS == PAIRS and PK <= P and FEAT_BATCHES % 2 == 1 and TURN_BATCHES % 2 == 0


def evens(n):
    return (n + 1) // 2


def odds(n):
    return n // 2


def pair_base(b):
    return b * (FEATS - 1) - b * (b - 1) // 2


def build(nc, dense, ids, tables, W1, b1, W2, b2, W3, out):
    with ExitStack() as ctx:
        def sb(name, shape, dt=F32):
            return ctx.enter_context(nc.sbuf_tensor(name, shape, dt))

        def ps(name, shape):
            return ctx.enter_context(nc.psum_tensor(name, shape, F32))

        def sem(name):
            return ctx.enter_context(nc.semaphore(name))

        idx = sb("idx", [P, GTILES, TABLES], I32)
        rows = sb("rows", [P, GTILES, FEATS, DIM])
        feats = sb("feats", [P, 2, P, FEATS_PAD])
        dots = sb("dots", [P, LEFT, GTILES * QT])
        pairs = sb("pairs", [P, LANES, PAIRS])
        pairs_t = sb("pairs_t", [PK, PCHUNKS, GCOLS])
        dense_t = sb("dense_t", [P, LANES, GTILES, QT])
        h1 = sb("h1", [P, H1 // P, GCOLS])
        h2 = sb("h2", [P, H2 // P, GCOLS])
        y = sb("y", [1, BATCH])
        ident = sb("ident", [P, P])
        w1_dense = sb("w1_dense", [P, H1])
        w1_dense2 = sb("w1_dense2", [P, H1])
        w1_pairs = sb("w1_pairs", [PK, PCHUNKS, H1])
        w2 = sb("w2", [P, H1 // P, H2])
        w3 = sb("w3", [P, H2 // P])
        bias1 = sb("bias1", [P, H1 // P])
        bias2 = sb("bias2", [P, H2 // P])

        feat_ps = [ps(f"feat_ps{k}", [P, TB, P]) for k in range(2)]
        dot_ps = [ps(f"dot_ps{k}", [P, 512]) for k in range(2)]
        turn_ps = [ps(f"turn_ps{k}", [P, TB, P]) for k in range(2)]
        mlp_ps = [ps(f"mlp_ps{k}", [P, GCOLS]) for k in range(2)]

        idx_in = [sem(f"idx_in{i}") for i in range(GTILES)]
        dense_in = [sem(f"dense_in{i}") for i in range(GTILES)]
        rows_in = [sem(f"rows_in{i}") for i in range(GTILES)]
        sp_passed = sem("sp_passed")
        pool_passed = sem("pool_passed")
        w1_in = sem("w1_in")
        w1p_in = sem("w1p_in")
        w2_in = sem("w2_in")
        small_in = sem("small_in")
        ident_zero = sem("ident_zero")
        ident_ready = sem("ident_ready")
        feats_zero = sem("feats_zero")
        w1_summed = sem("w1_summed")
        feat_done = sem("feat_done")
        dot_done = sem("dot_done")
        turn_done = sem("turn_done")
        mlp_done = sem("mlp_done")
        feat_out = [sem("feat_out_dve"), sem("feat_out_act")]
        dot_out = [sem("dot_out_dve"), sem("dot_out_act")]
        turn_out = [sem("turn_out_dve"), sem("turn_out_act")]
        mlp_out = [sem("mlp_out_dve"), sem("mlp_out_act")]
        y_out = sem("y_out")

        ids_v = ids.rearrange("(p g i) f -> p g i f", g=GROUPS, i=GTILES)
        dense_v = dense.rearrange("(p g i) d -> p g i d", g=GROUPS, i=GTILES)
        y_v = y[:, :].rearrange("o (j q g i) -> o g j i q", j=LANES, q=QT, g=GROUPS)

        block = ctx.enter_context(nc.Block())

        @block.sync
        def _(sp):
            def load_tile(g, i):
                sp.dma_start(idx[:, i, :], ids_v[:, g, i, :] if isinstance(g, int) else
                             ids_v[:, bass.ds(g, 1), i, :].rearrange("p g f -> p (g f)")).then_inc(idx_in[i], 16)
                sp.dma_start(rows[:, i, 0, :], dense_v[:, g, i, :] if isinstance(g, int) else
                             dense_v[:, bass.ds(g, 1), i, :].rearrange("p g d -> p (g d)")).then_inc(dense_in[i], 16)

            for i in range(GTILES):
                load_tile(0, i)
            sp.dma_start(w1_pairs[:, :, :], W1[DIM:DIM + PAIRS, :].rearrange("(c k) n -> k c n", c=PCHUNKS)).then_inc(w1p_in, 16)
            sp.dma_start(w2[:, :, :], W2.rearrange("(c k) n -> k c n", k=P)).then_inc(w2_in, 16)
            with sp.Fori(1, GROUPS) as g:
                for i in range(GTILES):
                    sp.wait_ge(feat_done, g * (GTILES * FEAT_BATCHES) + (i + 1 - GTILES) * FEAT_BATCHES)
                    sp.sem_inc(sp_passed, 1)
                    load_tile(g, i)
            sp.wait_ge(mlp_out[0], GROUPS * evens(MLP_STEPS) + 1)
            sp.dma_start(out.rearrange("(o s) one -> o (s one)", o=1), y[:, :]).then_inc(y_out, 16)
            sp.wait_ge(y_out, 16)

        @block.gpsimd
        def _(pool):
            def gather_tile(i):
                for f in range(TABLES):
                    pool.indirect_dma_start(
                        out=rows[:, i, 1 + f, :], out_offset=None, in_=tables[f][:, :],
                        in_offset=bass.IndirectOffsetOnAxis(ap=idx[:, i, f:f + 1].bitcast(U32), axis=0),
                    ).then_inc(rows_in[i], 16)

            for i in range(GTILES):
                pool.wait_ge(idx_in[i], 16)
                gather_tile(i)
                if i == 0:
                    nc.gpsimd.memset(ident[:, :], 0.0).then_inc(ident_zero, 1)
                    pool.wait_ge(ident_zero, 1)
                    nc.gpsimd.affine_select(out=ident[:, :], in_=ident[:, :], compare_op=ALU.not_equal, fill=1.0,
                                            base=0, pattern=[[-1, P]], channel_multiplier=1).then_inc(ident_ready, 1)
            with pool.Fori(1, GROUPS) as g:
                for i in range(GTILES):
                    pool.wait_ge(idx_in[i], (g + 1) * 16)
                    pool.wait_ge(feat_done, g * (GTILES * FEAT_BATCHES) + (i + 1 - GTILES) * FEAT_BATCHES)
                    pool.sem_inc(pool_passed, 1)
                    gather_tile(i)

        @block.tensor
        def _(pe):
            def feat_batch(g, i, b):
                n = i * FEAT_BATCHES + b
                k = n % 2
                if b == 0:
                    pe.wait_ge(dense_in[i], (g + 1) * 16)
                    pe.wait_ge(rows_in[i], (g + 1) * (16 * TABLES))
                pe.wait_ge(feat_out[k], g * (GTILES * FEAT_BATCHES // 2) + n // 2 + 1)
                for f in range(b * TB, min(b * TB + TB, FEATS)):
                    mm = pe.transpose(feat_ps[k][:, f % TB, :], rows[:, i, f, :], ident[:, :])
                mm.then_inc(feat_done, 1)

            def dot_half(g, i, half, feat_batches):
                pe.wait_ge(dot_out[half], g * GTILES + i + 1)
                batches = list(feat_batches)
                every = HALF_GRAMS // max(len(batches), 1)
                for n in range(HALF_GRAMS):
                    if batches and n % every == 0:
                        feat_batch(g, i + 1, batches.pop(0))
                    q, j = half * QH + n // LANES, n % LANES
                    x = feats[:, i % 2, j * QT + q, :]
                    mm = pe.matmul(dot_ps[half][FEATS_PAD * j:FEATS_PAD * (j + 1), (n // LANES) * LEFT:(n // LANES + 1) * LEFT],
                                   x, x[:, 0:LEFT], start=True, stop=True)
                mm.then_inc(dot_done, 1)

            pe.wait_ge(ident_ready, 1)
            pe.wait_ge(feats_zero, 1)
            pe.wait_ge(w1_summed, 1)
            pe.wait_ge(w1p_in, 16)
            pe.wait_ge(w2_in, 16)
            pe.wait_ge(small_in, 48)
            with pe.Fori(0, GROUPS) as g:
                for b in range(FEAT_BATCHES):
                    feat_batch(g, 0, b)
                for i in range(GTILES):
                    done = (i + 1) * FEAT_BATCHES
                    pe.wait_ge(feat_out[0], g * (GTILES * FEAT_BATCHES // 2) + evens(done) + 1)
                    pe.wait_ge(feat_out[1], g * (GTILES * FEAT_BATCHES // 2) + odds(done) + 1)
                    more = i + 1 < GTILES
                    dot_half(g, i, 0, range(BATCHES_EARLY) if more else [])
                    dot_half(g, i, 1, range(BATCHES_EARLY, FEAT_BATCHES) if more else [])
                pe.wait_ge(dot_out[0], (g + 1) * GTILES + 1)
                pe.wait_ge(dot_out[1], (g + 1) * GTILES + 1)
                for m in range(LEFT_BATCHES):
                    pe.wait_ge(turn_out[m % 2], g * (TURN_BATCHES // 2) + m // 2 + 1)
                    for b in range(m * TB, min(m * TB + TB, LEFT)):
                        mm = pe.transpose(turn_ps[m % 2][:, b % TB, :], dots[:, b, :], ident[:, :])
                    mm.then_inc(turn_done, 1)
                pe.wait_ge(turn_out[0], g * (TURN_BATCHES // 2) + evens(LEFT_BATCHES) + 1)
                pe.wait_ge(turn_out[1], g * (TURN_BATCHES // 2) + odds(LEFT_BATCHES) + 1)
                for c in range(PCHUNKS):
                    m = LEFT_BATCHES + c
                    pe.wait_ge(turn_out[m % 2], g * (TURN_BATCHES // 2) + m // 2 + 1)
                    for j in range(LANES):
                        mm = pe.transpose(turn_ps[m % 2][0:PK, j, :], pairs[:, j, c * PK:(c + 1) * PK], ident[:, :])
                    mm.then_inc(turn_done, 1)
                pe.wait_ge(turn_out[0], (g + 1) * (TURN_BATCHES // 2) + 1)
                pe.wait_ge(turn_out[1], (g + 1) * (TURN_BATCHES // 2) + 1)

                def bank_free(step):
                    per = evens(MLP_STEPS) if step % 2 == 0 else odds(MLP_STEPS)
                    pe.wait_ge(mlp_out[step % 2], g * per + step // 2 + 1)

                for n in range(H1 // P):
                    bank_free(n)
                    o, cols = mlp_ps[n % 2][:, :], slice(n * P, (n + 1) * P)
                    pe.matmul(o, w1_dense[:, cols], dense_t[:, :, :, :].rearrange("d j i q -> d (j i q)"), start=True, stop=False)
                    for c in range(PCHUNKS):
                        mm = pe.matmul(o, w1_pairs[:, c, cols], pairs_t[:, c, :], start=False, stop=(c == PCHUNKS - 1))
                    mm.then_inc(mlp_done, 1)
                pe.wait_ge(mlp_out[0], g * evens(MLP_STEPS) + evens(H1 // P) + 1)
                pe.wait_ge(mlp_out[1], g * odds(MLP_STEPS) + odds(H1 // P) + 1)
                for n in range(H2 // P):
                    s = H1 // P + n
                    for c in range(H1 // P):
                        mm = pe.matmul(mlp_ps[s % 2][:, :], w2[:, c, n * P:(n + 1) * P], h1[:, c, :], start=(c == 0), stop=(c == H1 // P - 1))
                    mm.then_inc(mlp_done, 1)
                s = MLP_STEPS - 1
                pe.wait_ge(mlp_out[0], g * evens(MLP_STEPS) + evens(s) + 1)
                pe.wait_ge(mlp_out[1], g * odds(MLP_STEPS) + odds(s) + 1)
                for c in range(H2 // P):
                    mm = pe.matmul(mlp_ps[s % 2][0:1, :], w3[:, c:c + 1], h2[:, c, :], start=(c == 0), stop=(c == H2 // P - 1))
                mm.then_inc(mlp_done, 1)

        def feat_views(i, b):
            n = min(TB, FEATS - b * TB)
            src = feat_ps[(i * FEAT_BATCHES + b) % 2]
            return (feats[:, i % 2, :, b * TB:b * TB + n].rearrange("d s f -> d f s"), src[:, 0:n, :],
                    dense_t[:, :, i, :], src[:, 0, :].rearrange("d (j q) -> d j q", j=LANES))

        def dot_views(i, half):
            return (dots[:, :, i * QT + half * QH:i * QT + (half + 1) * QH].rearrange("p b q -> p q b"),
                    dot_ps[half][:, 0:QH * LEFT].rearrange("p (q b) -> p q b", b=LEFT))

        def pair_views(b):
            src = turn_ps[(b // TB) % 2][:, b % TB, :].rearrange("p (j a) -> p j a", j=LANES)
            return pairs[:, :, pair_base(b):pair_base(b) + LEFT - b], src[:, :, b + 1:FEATS]

        def turn_views(c):
            return pairs_t[:, c, :], turn_ps[(LEFT_BATCHES + c) % 2][0:PK, :, :].rearrange("p j q -> p (j q)")

        @block.vector
        def _(dve):
            def features(g, i, batches):
                for b in batches:
                    n = i * FEAT_BATCHES + b
                    if n % 2 == 0:
                        dve.wait_ge(feat_done, g * (GTILES * FEAT_BATCHES) + n + 1)
                        to, src, dense_to, dense_src = feat_views(i, b)
                        if b == 0:
                            nc.vector.tensor_copy(dense_to, dense_src)
                        nc.vector.tensor_copy(to, src).then_inc(feat_out[0], 1)

            nc.vector.memset(feats[:, :, :, FEATS:FEATS_PAD], 0.0).then_inc(feats_zero, 1)
            dve.wait_ge(w1_in, 32)
            nc.vector.tensor_tensor(w1_dense[:, :], w1_dense[:, :], w1_dense2[:, :], ALU.add).then_inc(w1_summed, 1)
            for s in (feat_out, dot_out, turn_out, mlp_out):
                dve.sem_inc(s[0], 1)
            with dve.Fori(0, GROUPS) as g:
                features(g, 0, range(FEAT_BATCHES))
                for i in range(GTILES):
                    if i + 1 < GTILES:
                        features(g, i + 1, range(BATCHES_EARLY))
                    dve.wait_ge(dot_done, g * (2 * GTILES) + 2 * i + 1)
                    nc.vector.tensor_copy(*dot_views(i, 0)).then_inc(dot_out[0], 1)
                    if i + 1 < GTILES:
                        features(g, i + 1, range(BATCHES_EARLY, FEAT_BATCHES))
                for m in range(0, LEFT_BATCHES, 2):
                    dve.wait_ge(turn_done, g * TURN_BATCHES + m + 1)
                    for b in range(m * TB, min(m * TB + TB, LEFT)):
                        last = nc.vector.tensor_copy(*pair_views(b))
                    last.then_inc(turn_out[0], 1)
                dve.wait_ge(turn_done, g * TURN_BATCHES + LEFT_BATCHES + 2)
                nc.vector.tensor_copy(*turn_views(1)).then_inc(turn_out[0], 1)
                for s in range(0, MLP_STEPS, 2):
                    dve.wait_ge(mlp_done, g * MLP_STEPS + s + 1)
                    if s < MLP_STEPS - 1:
                        n = s - H1 // P
                        to, bias = (h1[:, s, :], bias1[:, s:s + 1]) if n < 0 else (h2[:, n, :], bias2[:, n:n + 1])
                        nc.vector.tensor_scalar(to, mlp_ps[0][:, :], bias, 0.0, ALU.add, ALU.max).then_inc(mlp_out[0], 1)
                nc.vector.tensor_copy(y_v[:, bass.ds(g, 1), :, :, :].rearrange("o g j i q -> o (g j) i q"),
                                      mlp_ps[0][0:1, :].rearrange("o (j i q) -> o j i q", j=LANES, i=GTILES)).then_inc(mlp_out[0], 1)

        @block.scalar
        def _(act):
            def features(g, i, batches):
                for b in batches:
                    n = i * FEAT_BATCHES + b
                    if n % 2 == 1:
                        act.wait_ge(feat_done, g * (GTILES * FEAT_BATCHES) + n + 1)
                        to, src, dense_to, dense_src = feat_views(i, b)
                        if b == 0:
                            nc.scalar.copy(dense_to, dense_src)
                        nc.scalar.copy(to, src).then_inc(feat_out[1], 1)

            act.dma_start(w1_dense[:, :], W1[0:DIM, :]).then_inc(w1_in, 16)
            act.dma_start(w1_dense2[:, :], W1[DIM + PAIRS:, :]).then_inc(w1_in, 16)
            with nc.allow_non_contiguous_dma(reason="1024 words of biases and of the last layer"):
                act.dma_start(bias1[:, :], b1.rearrange("(c p) -> p c", p=P)).then_inc(small_in, 16)
                act.dma_start(bias2[:, :], b2.rearrange("(c p) -> p c", p=P)).then_inc(small_in, 16)
                act.dma_start(w3[:, :], W3.rearrange("(c p) one -> p (c one)", p=P)).then_inc(small_in, 16)
            for s in (feat_out, dot_out, turn_out, mlp_out):
                act.sem_inc(s[1], 1)
            with act.Fori(0, GROUPS) as g:
                features(g, 0, range(FEAT_BATCHES))
                for i in range(GTILES):
                    if i + 1 < GTILES:
                        features(g, i + 1, range(FEAT_BATCHES))
                    act.wait_ge(dot_done, g * (2 * GTILES) + 2 * i + 2)
                    nc.scalar.copy(*dot_views(i, 1)).then_inc(dot_out[1], 1)
                for m in range(1, LEFT_BATCHES, 2):
                    act.wait_ge(turn_done, g * TURN_BATCHES + m + 1)
                    for b in range(m * TB, min(m * TB + TB, LEFT)):
                        last = nc.scalar.copy(*pair_views(b))
                    last.then_inc(turn_out[1], 1)
                for c in (0, 2):
                    act.wait_ge(turn_done, g * TURN_BATCHES + LEFT_BATCHES + c + 1)
                    nc.scalar.copy(*turn_views(c)).then_inc(turn_out[1], 1)
                for s in range(1, MLP_STEPS, 2):
                    act.wait_ge(mlp_done, g * MLP_STEPS + s + 1)
                    n = s - H1 // P
                    to, bias = (h1[:, s, :], bias1[:, s:s + 1]) if n < 0 else (h2[:, n, :], bias2[:, n:n + 1])
                    nc.scalar.activation(to, mlp_ps[1][:, :], ACT.Relu, bias=bias).then_inc(mlp_out[1], 1)


_TABLE_NAMES = [f"tbl_{f}" for f in range(TABLES)]


def kernel(**inputs):
    import numpy as _np
    import concourse.bacc as _bacc
    from concourse.bass_utils import run_bass_kernel_spmd as _run

    nc = _bacc.Bacc("TRN2", target_bir_lowering=False, num_devices=1)
    arrays, d = {}, {}
    for name in ["r_dense_features", "ids", *_TABLE_NAMES, "W_top1", "b_top1", "W_top2", "b_top2", "W_top3"]:
        a = _np.ascontiguousarray(inputs[name])
        arrays["in_" + name] = a
        d[name] = nc.dram_tensor("in_" + name, a.shape, mybir.dt.from_np(a.dtype), kind="ExternalInput").ap()
    out = nc.dram_tensor("out_y", (BATCH, 1), F32, kind="ExternalOutput").ap()
    build(nc, d["r_dense_features"], d["ids"], [d[t] for t in _TABLE_NAMES], d["W_top1"], d["b_top1"], d["W_top2"],
          d["b_top2"], d["W_top3"], out)
    return _run(nc, [arrays], core_ids=[0]).results[0]["out_y"]
```

```python
from contextlib import ExitStack

import concourse.bass as bass
from concourse import mybir

ALU = mybir.AluOpType
ACT = mybir.ActivationFunctionType
F32 = mybir.dt.float32
BF16 = mybir.dt.bfloat16
F32R = mybir.dt.float32r
I32 = mybir.dt.int32
U32 = mybir.dt.uint32

P = 128
BATCH = 2048
DIM = 128
TABLES = 26
FEATS = TABLES + 1
FEATS_PAD = 32
LEFT = FEATS - 1
PAIRS = FEATS * (FEATS - 1) // 2
H1, H2 = 512, 256

TILES = BATCH // P
DUOS = TILES // 2
COLS = 2 * P
LANES = 4
QT = P // LANES
QD = 2 * QT
QB = 4
DOT_BANKS = QT // QB

PICK_SETS = [(5, 6), (13, 14), (23, 24)]
PICKED = [f for s in PICK_SETS for f in s]
SETS = len(PICK_SETS)
PICKS = len(PICKED)
PICK_ROWS = 1000
PICK_CHUNKS = 8
PICK_K = PICK_ROWS // PICK_CHUNKS
PARTS = 2
HIGH_BITS = -(1 << 12)
GATHERED = [f for f in range(TABLES) if f not in PICKED]
SLOTS = [0] + [f + 1 for f in GATHERED]
ROW_BUFS = 4

TB = 4
FEAT_BATCHES = -(-len(SLOTS) // TB)
TURN_BATCHES = -(-(LEFT // 2) // TB)
PCHUNKS = 3
PK = PAIRS // PCHUNKS
L1_STEP = TURN_BATCHES + PCHUNKS
L2_STEP = L1_STEP + H1 // P
L3_STEP = L2_STEP + H2 // P
TAIL_STEPS = L3_STEP + 1
PICK_PIECES = 4
BUILD_PIECES = 4

assert PK * PCHUNKS == PAIRS and PICK_K * PICK_CHUNKS == PICK_ROWS
assert FEAT_BATCHES % 2 == 0 and TAIL_STEPS % 2 == 0 and LEFT % 2 == 0


def runs(features):
    found = []
    for at, f in enumerate(features):
        if found and f == found[-1][1] + found[-1][2]:
            found[-1][2] += 1
        else:
            found.append([at, f, 1])
    return found


def pair_base(b):
    return b * (FEATS - 1) - b * (b - 1) // 2


def build(nc, dense, ids, tables, W1, b1, W2, b2, W3, out):
    with ExitStack() as ctx:
        def sb(name, shape, dt=F32):
            return ctx.enter_context(nc.sbuf_tensor(name, shape, dt))

        def ps(name, shape):
            return ctx.enter_context(nc.psum_tensor(name, shape, F32))

        def sem(name):
            return ctx.enter_context(nc.semaphore(name))

        idx = sb("idx", [P, ROW_BUFS, TABLES], I32)
        rows = sb("rows", [P, ROW_BUFS, len(SLOTS), DIM])
        feats = sb("feats", [P, 2, P, FEATS_PAD])
        dots = sb("dots", [P, LEFT, QD])
        pairs = sb("pairs", [QD, LANES, PAIRS])
        pairs_t = sb("pairs_t", [PK, PCHUNKS, COLS])
        dense_t = sb("dense_t", [P, 2, LANES, 2, QT])
        h1 = sb("h1", [P, H1 // P, COLS])
        h2 = sb("h2", [P, H2 // P, COLS])
        narrow = sb("narrow", [P, BATCH])
        y = narrow[FEATS_PAD:FEATS_PAD + 1, :]
        ids_t = narrow[0:2 * PICKS, 0:BATCH // 2].bitcast(BF16)
        spread = narrow[0:2 * PICKS, BATCH // 2:BATCH // 2 + PICKS * P // 2].bitcast(BF16).rearrange("k (t p) -> k t p", t=PICKS)
        ident = sb("ident", [P, P])
        w1_dense = sb("w1_dense", [P, H1])
        w1_dense2 = h1[:, 0:2, :].rearrange("p c s -> p (c s)")
        w1_pairs = sb("w1_pairs", [PK, PCHUNKS, H1])
        w2 = sb("w2", [P, H1 // P, H2])
        w3 = sb("w3", [P, H2 // P])
        bias1 = sb("bias1", [P, H1 // P])
        bias2 = sb("bias2", [P, H2 // P])
        parts = sb("parts", [PICK_K, PICKS, PARTS, PICK_CHUNKS, DIM], F32R)
        onehot = sb("onehot", [PICK_K, 2, PICK_CHUNKS, 2 * COLS], F32R)
        stage = [feats[0:PICK_K, 0, n * QT:(n + 1) * QT, :].rearrange("k (c s) f -> k c (s f)", c=PICK_CHUNKS) for n in range(2)]
        high = [feats[0:PICK_K, 1, n * QT:(n + 1) * QT, :].rearrange("k (c s) f -> k c (s f)", c=PICK_CHUNKS) for n in range(2)]
        spare = dots[:, :, :].rearrange("p b q -> p (b q)")
        ids_all = spare[:, 0:TILES * TABLES].bitcast(I32).rearrange("p (t f) -> p t f", t=TILES)
        spare = spare[:, TILES * TABLES:]
        ids_hl = spare[:, 0:TILES * 2 * PICKS].rearrange("p (t f) -> p t f", t=TILES)
        ids_hi = spare[:, TILES * 2 * PICKS:TILES * 3 * PICKS].bitcast(BF16)[:, 0:TILES * PICKS].rearrange("p (t f) -> p t f", t=TILES)
        row_int = sb("row_int", [P, PICK_CHUNKS], I32)
        row_of = sb("row_of", [P, PICK_CHUNKS])

        feat_ps = [ps(f"feat_ps{k}", [P, TB, P]) for k in range(2)]
        dot_ps = [ps(f"dot_ps{k}", [P, QB, P]) for k in range(2)]
        tail_ps = [ps(f"tail_ps{k}", [P, TB, P]) for k in range(2)]
        ids_ps = ps("ids_ps", [P, 2 * COLS])
        pick_ps = ps("pick_ps", [P, 2, COLS])

        idx_in = [sem(f"idx_in{i}") for i in range(ROW_BUFS)]
        dense_in = [sem(f"dense_in{i}") for i in range(ROW_BUFS)]
        rows_in = [sem(f"rows_in{i}") for i in range(ROW_BUFS)]
        sp_passed = sem("sp_passed")
        pool_passed = sem("pool_passed")
        pe_passed = sem("pe_passed")
        w1_in = sem("w1_in")
        w1p_in = sem("w1p_in")
        w2_in = sem("w2_in")
        small_in = sem("small_in")
        ids_in = sem("ids_in")
        table_in = [sem(f"table_in{k}") for k in range(2)]
        ident_zero = sem("ident_zero")
        ident_ready = sem("ident_ready")
        spread_zero = sem("spread_zero")
        spread_half = sem("spread_half")
        spread_ready = sem("spread_ready")
        row_int_ready = sem("row_int_ready")
        row_of_ready = sem("row_of_ready")
        feats_zero = sem("feats_zero")
        w1_summed = sem("w1_summed")
        ids_hi_ready = sem("ids_hi_ready")
        ids_hl_ready = sem("ids_hl_ready")
        ids_turned = sem("ids_turned")
        ids_t_ready = sem("ids_t_ready")
        high_ready = sem("high_ready")
        high_cut = sem("high_cut")
        low_cut = sem("low_cut")
        feat_done = sem("feat_done")
        dot_done = sem("dot_done")
        tail_done = sem("tail_done")
        spread_done = sem("spread_done")
        pick_done = sem("pick_done")
        feat_out = [sem("feat_out_dve"), sem("feat_out_act")]
        dot_out = sem("dot_out")
        tail_out = [sem("tail_out_act"), sem("tail_out_dve")]
        onehot_ready = sem("onehot_ready")
        pick_out = sem("pick_out")
        y_out = sem("y_out")

        y_v = y.rearrange("o (u i q j) -> o u j i q", u=DUOS, i=2, j=LANES)
        ids_v = ids.rearrange("(g i p) f -> p g i f", p=P, i=ROW_BUFS)
        dense_v = dense.rearrange("(g i p) d -> p g i d", p=P, i=ROW_BUFS)

        block = ctx.enter_context(nc.Block())

        @block.sync
        def _(sp):
            def load_tile(g, i):
                sp.dma_start(idx[:, i, :], ids_v[:, g, i, :] if isinstance(g, int) else
                             ids_v[:, bass.ds(g, 1), i, :].rearrange("p g f -> p (g f)")).then_inc(idx_in[i], 16)
                sp.dma_start(rows[:, i, 0, :], dense_v[:, g, i, :] if isinstance(g, int) else
                             dense_v[:, bass.ds(g, 1), i, :].rearrange("p g d -> p (g d)")).then_inc(dense_in[i], 16)

            def load_table(n):
                if n >= 2:
                    sp.wait_ge(low_cut, n - 1)
                sp.dma_start(stage[n % 2], tables[PICKED[n]].rearrange("(k c) d -> k c d", c=PICK_CHUNKS)
                             ).then_inc(table_in[n % 2], 16)

            load_tile(0, 0)
            sp.dma_start(ids_all, ids.rearrange("(t p) f -> p t f", p=P)).then_inc(ids_in, 16)
            load_table(0)
            load_table(1)
            for i in range(1, ROW_BUFS):
                load_tile(0, i)
            for n in range(2, PICKS):
                load_table(n)
            sp.dma_start(w1_pairs[:, :, :], W1[DIM:DIM + PAIRS, :].rearrange("(c k) n -> k c n", c=PCHUNKS)).then_inc(w1p_in, 16)
            sp.dma_start(w2[:, :, :], W2.rearrange("(c k) n -> k c n", k=P)).then_inc(w2_in, 16)
            with sp.Fori(1, TILES // ROW_BUFS) as g:
                for i in range(ROW_BUFS):
                    sp.wait_ge(feat_done, g * (ROW_BUFS * FEAT_BATCHES) + (i + 1 - ROW_BUFS) * FEAT_BATCHES)
                    sp.sem_inc(sp_passed, 1)
                    load_tile(g, i)
            sp.wait_ge(tail_out[1], DUOS * (TAIL_STEPS // 2) + 1)
            sp.dma_start(out.rearrange("(o s) one -> o (s one)", o=1), y).then_inc(y_out, 16)
            sp.wait_ge(y_out, 16)

        @block.gpsimd
        def _(pool):
            def gather_tile(i):
                for slot, f in enumerate(GATHERED):
                    pool.indirect_dma_start(
                        out=rows[:, i, 1 + slot, :], out_offset=None, in_=tables[f][:, :],
                        in_offset=bass.IndirectOffsetOnAxis(ap=idx[:, i, f:f + 1].bitcast(U32), axis=0),
                    ).then_inc(rows_in[i], 16)

            nc.gpsimd.memset(ident[:, :], 0.0).then_inc(ident_zero, 1)
            nc.gpsimd.memset(spread, 0.0).then_inc(spread_zero, 1)
            nc.gpsimd.iota(row_int[:, :], pattern=[[1, PICK_CHUNKS]], base=0, channel_multiplier=PICK_CHUNKS
                           ).then_inc(row_int_ready, 1)
            pool.wait_ge(ident_zero, 1)
            nc.gpsimd.affine_select(out=ident[:, :], in_=ident[:, :], compare_op=ALU.not_equal, fill=1.0,
                                    base=0, pattern=[[-1, P]], channel_multiplier=1).then_inc(ident_ready, 1)
            for part, before, after in ((0, spread_zero, spread_half), (1, spread_half, spread_ready)):
                pool.wait_ge(before, 1)
                nc.gpsimd.affine_select(out=spread, in_=spread, compare_op=ALU.not_equal, fill=1.0,
                                        base=-part * PICKS, pattern=[[-1, PICKS], [0, P]], channel_multiplier=1
                                        ).then_inc(after, 1)
            for i in range(ROW_BUFS):
                pool.wait_ge(idx_in[i], 16)
                gather_tile(i)
            with pool.Fori(1, TILES // ROW_BUFS) as g:
                for i in range(ROW_BUFS):
                    pool.wait_ge(idx_in[i], (g + 1) * 16)
                    pool.wait_ge(feat_done, g * (ROW_BUFS * FEAT_BATCHES) + (i + 1 - ROW_BUFS) * FEAT_BATCHES)
                    pool.sem_inc(pool_passed, 1)
                    gather_tile(i)

        @block.tensor
        def _(pe):
            def feat_batch(g, buf, b):
                if b == 0:
                    pe.wait_ge(dense_in[buf], (g + 1) * 16)
                    pe.wait_ge(rows_in[buf], (g + 1) * (16 * len(GATHERED)))
                n = buf * FEAT_BATCHES + b
                pe.wait_ge(feat_out[b % 2], g * (ROW_BUFS * FEAT_BATCHES // 2) + n // 2 + 1)
                for s in range(b * TB, min(b * TB + TB, len(SLOTS))):
                    mm = pe.transpose(feat_ps[b % 2][:, s % TB, :], rows[:, buf, s, :], ident[:, :])
                mm.then_inc(feat_done, 1)

            def dot_tile(g, duo, i, next_tile):
                buf = 2 * duo + i
                pe.wait_ge(feat_out[0], g * (ROW_BUFS * FEAT_BATCHES // 2) + (buf + 1) * (FEAT_BATCHES // 2) + 1)
                pe.wait_ge(feat_out[1], g * (ROW_BUFS * FEAT_BATCHES // 2) + (buf + 1) * (FEAT_BATCHES // 2) + 1)
                pe.wait_ge(pick_out, g * (2 * SETS) + (duo + 1) * SETS + 1)
                for k in range(DOT_BANKS):
                    pe.wait_ge(dot_out, g * (ROW_BUFS * DOT_BANKS) + buf * DOT_BANKS + k + 1)
                    for n in range(QB):
                        x = feats[:, i, (k * QB + n) * LANES:(k * QB + n + 1) * LANES, :]
                        mm = pe.matmul(dot_ps[k % 2][:, n, 0:LANES * LEFT], x.rearrange("d s f -> d (s f)"),
                                       x[:, :, 0:LEFT], start=True, stop=True)
                    mm.then_inc(dot_done, 1)
                    if next_tile and k < FEAT_BATCHES:
                        feat_batch(*next_tile, k)

            def spread_ids(u, before, k):
                pe.wait_ge(onehot_ready, before + k + 1)
                pe.sem_inc(pe_passed, 1)
                for t in range(2):
                    cols = slice(u * COLS, (u + 1) * COLS) if isinstance(u, int) else bass.ds(u * COLS, COLS)
                    mm = pe.matmul(ids_ps[:, t * COLS:(t + 1) * COLS], spread[:, 2 * k + t, :], ids_t[:, cols],
                                   start=True, stop=True)
                mm.then_inc(spread_done, 1)

            def pick(duo, before, k, pieces=range(PICK_PIECES)):
                for piece in pieces:
                    if piece == 0:
                        pe.wait_ge(onehot_ready, before + k + 2)
                        pe.wait_ge(pick_out, before + k + 1)
                    t, half = piece // 2, piece % 2
                    for c in range(half * PICK_CHUNKS // 2, (half + 1) * PICK_CHUNKS // 2):
                        for part in range(PARTS):
                            mm = pe.matmul(pick_ps[:, t, :], parts[:, 2 * k + t, part, c, :],
                                           onehot[:, (duo * SETS + k) % 2, c, t * COLS:(t + 1) * COLS],
                                           start=(c == 0 and part == 0), stop=(c == PICK_CHUNKS - 1 and part == PARTS - 1))
                    if piece == PICK_PIECES - 1:
                        mm.then_inc(pick_done, 1)

            def tail_free(g, duo, step):
                pe.wait_ge(tail_out[step % 2], g * TAIL_STEPS + duo * (TAIL_STEPS // 2) + step // 2 + 1)

            def tail_whole(g, duo, steps):
                pe.wait_ge(tail_out[0], g * TAIL_STEPS + duo * (TAIL_STEPS // 2) + (steps + 1) // 2 + 1)
                pe.wait_ge(tail_out[1], g * TAIL_STEPS + duo * (TAIL_STEPS // 2) + steps // 2 + 1)

            def turn(g, duo, m):
                if m == 0:
                    pe.wait_ge(dot_out, g * (ROW_BUFS * DOT_BANKS) + 2 * (duo + 1) * DOT_BANKS + 2)
                tail_free(g, duo, m)
                for h in range(m * TB, min(m * TB + TB, LEFT // 2)):
                    mm = pe.transpose(tail_ps[m % 2][:, h % TB, :], dots[:, 2 * h:2 * h + 2, :], ident[:, :])
                mm.then_inc(tail_done, 1)

            def turn_back(g, duo, c):
                if c == 0:
                    tail_whole(g, duo, TURN_BATCHES)
                m = TURN_BATCHES + c
                tail_free(g, duo, m)
                pe.sem_inc(pe_passed, 1)
                to = tail_ps[m % 2][0:PK, :, :].rearrange("p t s -> p (t s)")
                for j in range(LANES):
                    mm = pe.transpose(to[:, j * QD:(j + 1) * QD], pairs[:, j, c * PK:(c + 1) * PK], ident[0:QD, 0:QD])
                mm.then_inc(tail_done, 1)

            def layer1(g, duo):
                tail_whole(g, duo, L1_STEP)
                for n in range(H1 // P):
                    m = L1_STEP + n
                    tail_free(g, duo, m)
                    to, cols = tail_ps[m % 2][:, 0:2, :], slice(n * P, (n + 1) * P)
                    pe.matmul(to, w1_dense[:, cols], dense_t[:, duo, :, :, :].rearrange("d j i q -> d (j i q)"), start=True, stop=False)
                    for c in range(PCHUNKS):
                        mm = pe.matmul(to, w1_pairs[:, c, cols], pairs_t[:, c, :], start=False, stop=(c == PCHUNKS - 1))
                    mm.then_inc(tail_done, 1)

            def layer2(g, duo):
                tail_whole(g, duo, L2_STEP)
                for n in range(H2 // P):
                    m = L2_STEP + n
                    for c in range(H1 // P):
                        mm = pe.matmul(tail_ps[m % 2][:, 0:2, :], w2[:, c, n * P:(n + 1) * P], h1[:, c, :],
                                       start=(c == 0), stop=(c == H1 // P - 1))
                    mm.then_inc(tail_done, 1)

            def layer3(g, duo):
                tail_whole(g, duo, L3_STEP)
                for c in range(H2 // P):
                    mm = pe.matmul(tail_ps[L3_STEP % 2][0:1, 0:2, :], w3[:, c:c + 1], h2[:, c, :],
                                   start=(c == 0), stop=(c == H2 // P - 1))
                mm.then_inc(tail_done, 1)

            def step(g, duo, ahead):
                u, other, before = g * 2 + duo + 1, 1 - duo, g * (2 * SETS) + (duo + 1) * SETS

                def picks(k, *pieces):
                    if ahead:
                        pick(other, before, k, pieces)

                if ahead:
                    spread_ids(u, before, 0)
                dot_tile(g, duo, 0, (g, 2 * duo + 1))
                if ahead:
                    spread_ids(u, before, 1)
                dot_tile(g, duo, 1, (g + duo, 2 * other) if ahead else None)
                if ahead:
                    spread_ids(u, before, 2)
                picks(0, 0, 1)
                turn(g, duo, 0)
                turn(g, duo, 1)
                picks(0, 2)
                turn(g, duo, 2)
                turn(g, duo, 3)
                picks(0, 3)
                turn_back(g, duo, 0)
                turn_back(g, duo, 1)
                picks(1, 0)
                turn_back(g, duo, 2)
                picks(1, 1, 2)
                layer1(g, duo)
                picks(1, 3)
                layer2(g, duo)
                picks(2, 0, 1, 2, 3)
                layer3(g, duo)

            pe.sem_inc(pick_done, 2)
            pe.wait_ge(ident_ready, 1)
            pe.wait_ge(ids_hl_ready, 2)
            for m in range(TILES // TB):
                if m >= 2:
                    pe.wait_ge(ids_t_ready, m - 1)
                for t in range(TB):
                    mm = pe.transpose(tail_ps[m % 2][0:2 * PICKS, t, :], ids_hl[:, m * TB + t, :], ident[:, :])
                mm.then_inc(ids_turned, 1)
            pe.wait_ge(ids_t_ready, TILES // TB)
            pe.wait_ge(spread_ready, 1)
            spread_ids(0, 0, 0)
            for k in range(SETS):
                if k + 1 < SETS:
                    spread_ids(0, 0, k + 1)
                pe.wait_ge(high_cut, 2 * (k + 1))
                pe.wait_ge(low_cut, 2 * (k + 1))
                pick(0, 0, k)
            pe.wait_ge(feats_zero, 1)
            pe.wait_ge(w1_summed, 1)
            pe.wait_ge(w1p_in, 16)
            pe.wait_ge(w2_in, 16)
            pe.wait_ge(small_in, 48)
            for b in range(FEAT_BATCHES):
                feat_batch(0, 0, b)
            with pe.Fori(0, DUOS // 2 - 1) as g:
                step(g, 0, True)
                step(g, 1, True)
            step(DUOS // 2 - 1, 0, True)
            step(DUOS // 2 - 1, 1, False)

        def feat_views(i, b):
            features = SLOTS[b * TB:b * TB + TB]
            for at, f, n in runs(features):
                yield feats[:, i, :, f:f + n].rearrange("d s f -> d f s"), feat_ps[b % 2][:, at:at + n, :]

        def dot_views(i, k, j):
            at, low = i * QT + k * QB, FEATS_PAD * j
            return (dots[low:low + FEATS_PAD, :, at:at + QB],
                    dot_ps[k % 2][low:low + FEATS_PAD, :, j * LEFT:(j + 1) * LEFT].rearrange("a n b -> a b n"))

        def turn_views(m):
            for b in range(2 * m * TB, min(2 * m * TB + 2 * TB, LEFT)):
                low = QD * (b % 2)
                src = tail_ps[m % 2][low:low + QD, (b // 2) % TB, :].rearrange("p (j a) -> p j a", j=LANES)
                yield pairs[:, :, pair_base(b):pair_base(b) + LEFT - b], src[:, :, b + 1:FEATS]

        def turn_back_views(m):
            return pairs_t[:, m - TURN_BATCHES, :], tail_ps[m % 2][0:PK, 0:2, :].rearrange("p t s -> p (t s)")

        def layer_views(m):
            src = tail_ps[m % 2][:, 0:2, :].rearrange("p t s -> p (t s)")
            if m < L2_STEP:
                n = m - L1_STEP
                return h1[:, n, :], src, bias1[:, n:n + 1]
            n = m - L2_STEP
            return h2[:, n, :], src, bias2[:, n:n + 1]

        @block.vector
        def _(dve):
            def features(g, buf, b):
                dve.wait_ge(feat_done, g * (ROW_BUFS * FEAT_BATCHES) + buf * FEAT_BATCHES + b + 1)
                i = buf % 2
                if b == 0:
                    nc.vector.tensor_copy(dense_t[:, buf // 2, :, i, :], feat_ps[0][:, 0, :].rearrange("d (q j) -> d j q", j=LANES))
                for to, src in feat_views(i, b):
                    last = nc.vector.tensor_copy(to, src)
                last.then_inc(feat_out[0], 1)

            def build_onehot(duo, before, k, chunks=range(PICK_CHUNKS)):
                for c in chunks:
                    if c == 0:
                        dve.wait_ge(spread_done, before + k + 1)
                        dve.wait_ge(pick_done, before + k + 1)
                    last = nc.vector.tensor_scalar(onehot[:, (duo * SETS + k) % 2, c, :], ids_ps[0:PICK_K, :],
                                                   row_of[0:PICK_K, c:c + 1], None, ALU.is_equal)
                    if c == PICK_CHUNKS - 1:
                        last.then_inc(onehot_ready, 1)

            def tail(g, duo, m):
                dve.wait_ge(tail_done, g * (2 * TAIL_STEPS) + duo * TAIL_STEPS + m + 1)
                if m < TURN_BATCHES:
                    for to, src in turn_views(m):
                        last = nc.vector.tensor_copy(to, src)
                elif m < L1_STEP:
                    last = nc.vector.tensor_copy(*turn_back_views(m))
                elif m < L3_STEP:
                    to, src, bias = layer_views(m)
                    last = nc.vector.tensor_scalar(to, src, bias, 0.0, ALU.add, ALU.max)
                else:
                    u = g * 2 + duo
                    to = y_v[:, u, :, :, :] if isinstance(u, int) else \
                        y_v[:, bass.ds(u, 1), :, :, :].rearrange("o u j i q -> o (u j) i q")
                    src = tail_ps[m % 2][0:1, 0:2, :].rearrange("o t s -> o (t s)")
                    last = nc.vector.tensor_copy(to, src.rearrange("o (j i q) -> o j i q", j=LANES, i=2))
                last.then_inc(tail_out[1], 1)

            def step(g, duo, ahead):
                other, before = 1 - duo, g * (2 * SETS) + (duo + 1) * SETS
                for i, follows in ((0, (g, 2 * duo + 1)), (1, (g + duo, 2 * other) if ahead else None)):
                    for b in range(0, FEAT_BATCHES, 2):
                        if follows:
                            features(*follows, b)
                        if ahead:
                            build_onehot(other, before, i, range(b * PICK_CHUNKS // FEAT_BATCHES, (b + 2) * PICK_CHUNKS // FEAT_BATCHES))
                for m in range(1, TAIL_STEPS, 2):
                    tail(g, duo, m)
                    piece = (m - TURN_BATCHES + 1) // 2
                    if ahead and 0 <= piece < BUILD_PIECES:
                        build_onehot(other, before, 2, range(piece * PICK_CHUNKS // BUILD_PIECES, (piece + 1) * PICK_CHUNKS // BUILD_PIECES))

            for s in (feat_out[0], tail_out[1], onehot_ready):
                dve.sem_inc(s, 1)
            dve.wait_ge(row_int_ready, 1)
            nc.vector.tensor_copy(row_of[:, :], row_int[:, :]).then_inc(row_of_ready, 1)
            dve.wait_ge(ids_in, 16)
            for k, (f, _) in enumerate(PICK_SETS):
                last = nc.vector.tensor_copy(ids_hi[:, :, 2 * k:2 * k + 2], ids_all[:, :, f:f + 2])
            last.then_inc(ids_hi_ready, 1)
            dve.wait_ge(ids_hi_ready, 1)
            nc.vector.tensor_copy(ids_hl[:, :, 0:PICKS], ids_hi[:, :, :]).then_inc(ids_hl_ready, 1)
            for k, (f, _) in enumerate(PICK_SETS):
                last = nc.vector.tensor_tensor(ids_hl[:, :, PICKS + 2 * k:PICKS + 2 * k + 2], ids_all[:, :, f:f + 2],
                                               ids_hi[:, :, 2 * k:2 * k + 2], ALU.subtract)
            last.then_inc(ids_hl_ready, 1)
            for m in range(TILES // TB):
                dve.wait_ge(ids_turned, m + 1)
                nc.vector.tensor_copy(ids_t[:, m * TB * P:(m + 1) * TB * P],
                                      tail_ps[m % 2][0:2 * PICKS, :, :].rearrange("p t s -> p (t s)")).then_inc(ids_t_ready, 1)
            dve.wait_ge(row_of_ready, 1)
            for k in range(SETS):
                build_onehot(0, 0, k)
                for n in (2 * k, 2 * k + 1):
                    dve.wait_ge(table_in[n % 2], 16 * (k + 1))
                    if k:
                        dve.wait_ge(high_cut, n - 1)
                        dve.wait_ge(low_cut, n - 1)
                    nc.vector.tensor_scalar(high[n % 2].bitcast(I32), stage[n % 2].bitcast(I32), HIGH_BITS, None,
                                            ALU.bitwise_and).then_inc(high_ready, 1)
                for n in (2 * k, 2 * k + 1):
                    dve.wait_ge(high_ready, n + 1)
                    nc.vector.tensor_tensor(parts[:, n, 1, :, :], stage[n % 2], high[n % 2], ALU.subtract).then_inc(low_cut, 1)
            dve.wait_ge(low_cut, PICKS)
            dve.wait_ge(high_cut, PICKS)
            nc.vector.memset(feats[:, :, :, FEATS:FEATS_PAD], 0.0).then_inc(feats_zero, 1)
            dve.wait_ge(w1_in, 32)
            nc.vector.tensor_tensor(w1_dense[:, :], w1_dense[:, :], w1_dense2, ALU.add).then_inc(w1_summed, 1)
            for b in range(0, FEAT_BATCHES, 2):
                features(0, 0, b)
            with dve.Fori(0, DUOS // 2 - 1) as g:
                step(g, 0, True)
                step(g, 1, True)
            step(DUOS // 2 - 1, 0, True)
            step(DUOS // 2 - 1, 1, False)

        @block.scalar
        def _(act):
            def features(g, buf, b):
                act.wait_ge(feat_done, g * (ROW_BUFS * FEAT_BATCHES) + buf * FEAT_BATCHES + b + 1)
                for to, src in feat_views(buf % 2, b):
                    last = nc.scalar.copy(to, src)
                last.then_inc(feat_out[1], 1)

            def tile_dots(g, duo, i, next_tile):
                for k in range(DOT_BANKS):
                    act.wait_ge(dot_done, g * (ROW_BUFS * DOT_BANKS) + (2 * duo + i) * DOT_BANKS + k + 1)
                    for j in range(LANES):
                        last = nc.scalar.copy(*dot_views(i, k, j))
                    last.then_inc(dot_out, 1)
                    if next_tile and k < FEAT_BATCHES and k % 2 == 1:
                        features(*next_tile, k)

            def picked(before, k):
                act.wait_ge(pick_done, before + k + 3)
                f = 1 + PICK_SETS[k][0]
                nc.scalar.copy(feats[:, :, :, f:f + 2].rearrange("d i s f -> d f i s"),
                               pick_ps[:, :, :].rearrange("d f (i s) -> d f i s", i=2)).then_inc(pick_out, 1)

            def tail(g, duo, *steps):
                for m in steps:
                    act.wait_ge(tail_done, g * (2 * TAIL_STEPS) + duo * TAIL_STEPS + m + 1)
                    if m < TURN_BATCHES:
                        for to, src in turn_views(m):
                            last = nc.scalar.copy(to, src)
                    elif m < L1_STEP:
                        last = nc.scalar.copy(*turn_back_views(m))
                    else:
                        to, src, bias = layer_views(m)
                        last = nc.scalar.activation(to, src, ACT.Relu, bias=bias)
                    last.then_inc(tail_out[0], 1)

            def step(g, duo, ahead):
                before = g * (2 * SETS) + (duo + 1) * SETS
                tile_dots(g, duo, 0, (g, 2 * duo + 1))
                tile_dots(g, duo, 1, (g + duo, 2 - 2 * duo) if ahead else None)
                tail(g, duo, 0, 2)
                if ahead:
                    picked(before, 0)
                tail(g, duo, 4, 6, 8, 10)
                if ahead:
                    picked(before, 1)
                tail(g, duo, 12)
                if ahead:
                    picked(before, 2)

            act.dma_start(w1_dense[:, :], W1[0:DIM, :]).then_inc(w1_in, 16)
            act.dma_start(w1_dense2, W1[DIM + PAIRS:, :]).then_inc(w1_in, 16)
            with nc.allow_non_contiguous_dma(reason="1024 words of biases and of the last layer"):
                act.dma_start(bias1[:, :], b1.rearrange("(c p) -> p c", p=P)).then_inc(small_in, 16)
                act.dma_start(bias2[:, :], b2.rearrange("(c p) -> p c", p=P)).then_inc(small_in, 16)
                act.dma_start(w3[:, :], W3.rearrange("(c p) one -> p (c one)", p=P)).then_inc(small_in, 16)
            for s, n in ((feat_out[1], 1), (dot_out, 2), (tail_out[0], 1), (pick_out, 1)):
                act.sem_inc(s, n)
            for n in range(PICKS):
                act.wait_ge(high_ready, n + 1)
                nc.scalar.copy(parts[:, n, 0, :, :], high[n % 2]).then_inc(high_cut, 1)
            act.wait_ge(feats_zero, 1)
            for k in range(SETS):
                picked(0, k)
            for b in range(1, FEAT_BATCHES, 2):
                features(0, 0, b)
            with act.Fori(0, DUOS // 2 - 1) as g:
                step(g, 0, True)
                step(g, 1, True)
            step(DUOS // 2 - 1, 0, True)
            step(DUOS // 2 - 1, 1, False)


_TABLE_NAMES = [f"tbl_{f}" for f in range(TABLES)]


def kernel(**inputs):
    import numpy as _np
    import concourse.bacc as _bacc
    from concourse.bass_utils import run_bass_kernel_spmd as _run

    nc = _bacc.Bacc("TRN2", target_bir_lowering=False, num_devices=1)
    arrays, d = {}, {}
    for name in ["r_dense_features", "ids", *_TABLE_NAMES, "W_top1", "b_top1", "W_top2", "b_top2", "W_top3"]:
        a = _np.ascontiguousarray(inputs[name])
        arrays["in_" + name] = a
        d[name] = nc.dram_tensor("in_" + name, a.shape, mybir.dt.from_np(a.dtype), kind="ExternalInput").ap()
    out = nc.dram_tensor("out_y", (BATCH, 1), F32, kind="ExternalOutput").ap()
    build(nc, d["r_dense_features"], d["ids"], [d[t] for t in _TABLE_NAMES], d["W_top1"], d["b_top1"], d["W_top2"],
          d["b_top2"], d["W_top3"], out)
    return _run(nc, [arrays], core_ids=[0]).results[0]["out_y"]
```

```python
from contextlib import ExitStack

import concourse.bass as bass
from concourse import mybir

ALU = mybir.AluOpType
ACT = mybir.ActivationFunctionType
F32 = mybir.dt.float32
BF16 = mybir.dt.bfloat16
F32R = mybir.dt.float32r
I32 = mybir.dt.int32
U32 = mybir.dt.uint32

P = 128
BATCH = 2048
DIM = 128
TABLES = 26
FEATS = TABLES + 1
FEATS_PAD = 32
LEFT = FEATS - 1
PAIRS = FEATS * (FEATS - 1) // 2
H1, H2 = 512, 256

TILES = BATCH // P
DUOS = TILES // 2
GROUPS = DUOS // 2
COLS = 2 * P
LANES = 4
QT = P // LANES
QD = 2 * QT
QB = 4
DOT_BANKS = QT // QB
STAT = (LANES - 1) * FEATS_PAD + LEFT

PICK_SETS = [(5, 6), (13, 14), (23, 24)]
PICKED = [f for s in PICK_SETS for f in s]
SETS = len(PICK_SETS)
PICKS = len(PICKED)
PICK_ROWS = 1000
PICK_CHUNKS = 8
PICK_K = PICK_ROWS // PICK_CHUNKS
PARTS = 2
HIGH_BITS = -(1 << 12)
GATHERED = [f for f in range(TABLES) if f not in PICKED]
SLOTS = [0] + [f + 1 for f in GATHERED]
ROW_BUFS = 4

TB = 4
FEAT_BATCHES = -(-len(SLOTS) // TB)
TURN_BATCHES = -(-(LEFT // 2) // TB)
PCHUNKS = 3
PK = PAIRS // PCHUNKS
L1_STEP = TURN_BATCHES + PCHUNKS
L2_STEP = L1_STEP + H1 // P
L3_STEP = L2_STEP + H2 // P
TAIL_STEPS = L3_STEP + 1
PICK_PIECES = 8
DVE_CHUNKS = 4
ACT_CHUNKS = PICK_CHUNKS - DVE_CHUNKS
FEATS_AFTER = (2, 2, 4, 4, 6, 6)
SPARED = (2, 3, TURN_BATCHES + 2, *range(L1_STEP, L2_STEP))
BUILD_AFTER = (1, 3, 6, 7)
BUILD_PIECE = PICK_CHUNKS // len(BUILD_AFTER)

assert PK * PCHUNKS == PAIRS and PICK_K * PICK_CHUNKS == PICK_ROWS
assert FEAT_BATCHES % 2 == 0 and TAIL_STEPS % 2 == 0 and LEFT % 2 == 0


def runs(features):
    found = []
    for at, f in enumerate(features):
        if found and f == found[-1][1] + found[-1][2]:
            found[-1][2] += 1
        else:
            found.append([at, f, 1])
    return found


def pair_base(b):
    return b * (FEATS - 1) - b * (b - 1) // 2


def turned_for(c):
    return 1 + max(b for b in range(LEFT) if pair_base(b) < (c + 1) * PK) // (2 * TB)


def emptied(steps, parity):
    return len([m for m in range(steps) if m % 2 == parity and not TURN_BATCHES <= m < L1_STEP])


def build(nc, dense, ids, tables, W1, b1, W2, b2, W3, out):
    with ExitStack() as ctx:
        def sb(name, shape, dt=F32):
            return ctx.enter_context(nc.sbuf_tensor(name, shape, dt))

        def ps(name, shape):
            return ctx.enter_context(nc.psum_tensor(name, shape, F32))

        def sem(name):
            return ctx.enter_context(nc.semaphore(name))

        idx = sb("idx", [P, ROW_BUFS, TABLES], I32)
        rows = sb("rows", [P, ROW_BUFS, len(SLOTS), DIM])
        feats = sb("feats", [P, 2, P, FEATS_PAD])
        dots = sb("dots", [P, LEFT, QD])
        pairs = sb("pairs", [QD, LANES, PAIRS])
        pairs_hi = sb("pairs_hi", [PK, PCHUNKS, COLS], F32R)
        pairs_lo = sb("pairs_lo", [PK, PCHUNKS, COLS], F32R)
        dense_t = sb("dense_t", [P, 2, LANES, 2, QT])
        h1 = sb("h1", [P, H1 // P, COLS])
        h2 = sb("h2", [P, H2 // P, COLS])
        narrow = sb("narrow", [P, BATCH])
        y = narrow[FEATS_PAD:FEATS_PAD + 1, :]
        ids_t = narrow[0:2 * PICKS, 0:BATCH // 2].bitcast(BF16)
        spread = narrow[0:2 * PICKS, BATCH // 2:BATCH // 2 + PICKS * P // 2].bitcast(BF16).rearrange("k (t p) -> k t p", t=PICKS)
        ident = sb("ident", [P, P])
        w1_dense = sb("w1_dense", [P, H1])
        w1_dense2 = h1[:, 0:2, :].rearrange("p c s -> p (c s)")
        w1_hi = sb("w1_hi", [PK, PCHUNKS, H1], F32R)
        w1_lo = sb("w1_lo", [PK, PCHUNKS, H1], F32R)
        w2 = sb("w2", [P, H1 // P, H2])
        w3 = sb("w3", [P, H2 // P])
        bias1 = sb("bias1", [P, H1 // P])
        bias2 = sb("bias2", [P, H2 // P])
        parts = sb("parts", [PICK_K, PICKS, PARTS, PICK_CHUNKS, DIM], F32R)
        onehot = sb("onehot", [PICK_K, 2, PICK_CHUNKS, 2 * COLS], F32R)
        stage = [feats[0:PICK_K, 1, n * QT:(n + 1) * QT, :].rearrange("k (c s) f -> k c (s f)", c=PICK_CHUNKS) for n in range(4)]
        stage += [rows[0:PICK_K, 3, n * PICK_CHUNKS:(n + 1) * PICK_CHUNKS, :] for n in range(2)]
        high = [rows[0:PICK_K, 2, n * PICK_CHUNKS:(n + 1) * PICK_CHUNKS, :] for n in range(2)]
        apart = [h1[0:PICK_K, 2:4, :].rearrange("k c s -> k (c s)"), h2[0:PICK_K, 0:2, :].rearrange("k c s -> k (c s)")]
        spare = dots[:, :, :].rearrange("p b q -> p (b q)")
        ids_all = spare[:, 0:TILES * TABLES].bitcast(I32).rearrange("p (t f) -> p t f", t=TILES)
        spare = spare[:, TILES * TABLES:]
        ids_hl = spare[:, 0:TILES * 2 * PICKS].rearrange("p (t f) -> p t f", t=TILES)
        ids_hi = spare[:, TILES * 2 * PICKS:TILES * 3 * PICKS].bitcast(BF16)[:, 0:TILES * PICKS].rearrange("p (t f) -> p t f", t=TILES)
        spare = spare[:, TILES * 3 * PICKS:]
        w1_stage = [rows[0:PK, i, 2 * PICK_CHUNKS:2 * PICK_CHUNKS + H1 // DIM, :].rearrange("k c d -> k (c d)") for i in (2, 3)]
        w1_stage += [spare[0:PK, 0:H1]]
        pairs_masked = h2[0:PK, :, :]
        row_int = sb("row_int", [P, PICK_CHUNKS], I32)
        row_of = sb("row_of", [P, PICK_CHUNKS])
        minus_row = sb("minus_row", [P, PICK_CHUNKS])

        feat_ps = [ps(f"feat_ps{k}", [P, TB, P]) for k in range(2)]
        dot_ps = [ps(f"dot_ps{k}", [P, QB, P]) for k in range(2)]
        tail_ps = [ps(f"tail_ps{k}", [P, TB, P]) for k in range(2)]
        ids_ps = ps("ids_ps", [P, 2 * COLS])
        pick_ps = ps("pick_ps", [P, 2, COLS])

        idx_in = [sem(f"idx_in{i}") for i in range(ROW_BUFS)]
        dense_in = [sem(f"dense_in{i}") for i in range(ROW_BUFS)]
        rows_in = [sem(f"rows_in{i}") for i in range(ROW_BUFS)]
        sp_passed = sem("sp_passed")
        pool_passed = sem("pool_passed")
        dve_passed = sem("dve_passed")
        pe_passed = sem("pe_passed")
        w1_in = sem("w1_in")
        w1p_in = sem("w1p_in")
        w2_in = sem("w2_in")
        small_in = sem("small_in")
        ids_in = sem("ids_in")
        table_in = [sem(f"table_in{n}") for n in range(PICKS)]
        ident_zero = sem("ident_zero")
        ident_ready = sem("ident_ready")
        spread_zero = sem("spread_zero")
        spread_half = sem("spread_half")
        spread_ready = sem("spread_ready")
        row_int_ready = sem("row_int_ready")
        row_of_ready = sem("row_of_ready")
        minus_row_ready = sem("minus_row_ready")
        apart_ready = sem("apart_ready")
        act_onehot_ready = sem("act_onehot_ready")
        feats_zero = sem("feats_zero")
        w1_summed = sem("w1_summed")
        w1_masked = sem("w1_masked")
        w1_hi_ready = sem("w1_hi_ready")
        w1_lo_ready = sem("w1_lo_ready")
        pairs_mask_ready = sem("pairs_mask_ready")
        pairs_hi_ready = sem("pairs_hi_ready")
        pairs_lo_ready = sem("pairs_lo_ready")
        ids_hi_ready = sem("ids_hi_ready")
        ids_hl_ready = sem("ids_hl_ready")
        ids_turned = sem("ids_turned")
        ids_t_ready = sem("ids_t_ready")
        high_ready = sem("high_ready")
        high_cut = sem("high_cut")
        low_cut = sem("low_cut")
        feat_done = sem("feat_done")
        dot_done = sem("dot_done")
        tail_done = sem("tail_done")
        spread_done = sem("spread_done")
        act_spread_done = sem("act_spread_done")
        pick_done = sem("pick_done")
        feat_out = [sem("feat_out_dve"), sem("feat_out_act")]
        dot_out = sem("dot_out")
        tail_out = [sem("tail_out_act"), sem("tail_out_dve")]
        onehot_ready = sem("onehot_ready")
        pick_out = sem("pick_out")
        y_out = sem("y_out")

        y_v = y.rearrange("o (u i q j) -> o u j i q", u=DUOS, i=2, j=LANES)
        ids_v = ids.rearrange("(g i p) f -> p g i f", p=P, i=ROW_BUFS)
        dense_v = dense.rearrange("(g i p) d -> p g i d", p=P, i=ROW_BUFS)

        def tail_bank(m, ahead):
            if ahead or m not in SPARED:
                return tail_ps[m % 2]
            if m < L1_STEP:
                return feat_ps[m % 2]
            return [dot_ps[0], dot_ps[1], ids_ps[:, :].rearrange("p (t s) -> p t s", t=TB),
                    pick_ps[:, :, :].rearrange("p f (t s) -> p (f t) s", s=P)][m - L1_STEP]

        block = ctx.enter_context(nc.Block())

        @block.sync
        def _(sp):
            def load_tile(g, i):
                sp.dma_start(idx[:, i, :], ids_v[:, g, i, :] if isinstance(g, int) else
                             ids_v[:, bass.ds(g, 1), i, :].rearrange("p g f -> p (g f)")).then_inc(idx_in[i], 16)
                sp.dma_start(rows[:, i, 0, :], dense_v[:, g, i, :] if isinstance(g, int) else
                             dense_v[:, bass.ds(g, 1), i, :].rearrange("p g d -> p (g d)")).then_inc(dense_in[i], 16)

            def load_table(n):
                sp.dma_start(stage[n], tables[PICKED[n]].rearrange("(k c) d -> k c d", c=PICK_CHUNKS)).then_inc(table_in[n], 16)

            load_tile(0, 0)
            sp.dma_start(ids_all, ids.rearrange("(t p) f -> p t f", p=P)).then_inc(ids_in, 16)
            for n in range(PICKS):
                load_table(n)
                if n == 0:
                    load_tile(0, 1)
            for c in range(PCHUNKS):
                sp.dma_start(w1_stage[c], W1[DIM + c * PK:DIM + (c + 1) * PK, :]).then_inc(w1p_in, 16)
            sp.dma_start(w2[:, :, :], W2.rearrange("(c k) n -> k c n", k=P)).then_inc(w2_in, 16)
            sp.wait_ge(low_cut, PICKS)
            sp.wait_ge(high_cut, PICKS)
            sp.wait_ge(w1_lo_ready, 2)
            for i in range(2, ROW_BUFS):
                load_tile(0, i)
            with sp.Fori(1, TILES // ROW_BUFS) as g:
                for i in range(ROW_BUFS):
                    sp.wait_ge(feat_done, g * (ROW_BUFS * FEAT_BATCHES) + (i + 1 - ROW_BUFS) * FEAT_BATCHES)
                    sp.sem_inc(sp_passed, 1)
                    load_tile(g, i)
            sp.wait_ge(tail_out[1], DUOS * emptied(TAIL_STEPS, 1) + 1)
            sp.dma_start(out.rearrange("(o s) one -> o (s one)", o=1), y).then_inc(y_out, 16)
            sp.wait_ge(y_out, 16)

        @block.gpsimd
        def _(pool):
            def gather_tile(i):
                for slot, f in enumerate(GATHERED):
                    pool.indirect_dma_start(
                        out=rows[:, i, 1 + slot, :], out_offset=None, in_=tables[f][:, :],
                        in_offset=bass.IndirectOffsetOnAxis(ap=idx[:, i, f:f + 1].bitcast(U32), axis=0),
                    ).then_inc(rows_in[i], 16)

            nc.gpsimd.memset(ident[:, :], 0.0).then_inc(ident_zero, 1)
            nc.gpsimd.memset(spread, 0.0).then_inc(spread_zero, 1)
            nc.gpsimd.iota(row_int[:, :], pattern=[[1, PICK_CHUNKS]], base=0, channel_multiplier=PICK_CHUNKS
                           ).then_inc(row_int_ready, 1)
            pool.wait_ge(ident_zero, 1)
            nc.gpsimd.affine_select(out=ident[:, :], in_=ident[:, :], compare_op=ALU.not_equal, fill=1.0,
                                    base=0, pattern=[[-1, P]], channel_multiplier=1).then_inc(ident_ready, 1)
            for part, before, after in ((0, spread_zero, spread_half), (1, spread_half, spread_ready)):
                pool.wait_ge(before, 1)
                nc.gpsimd.affine_select(out=spread, in_=spread, compare_op=ALU.not_equal, fill=1.0,
                                        base=-part * PICKS, pattern=[[-1, PICKS], [0, P]], channel_multiplier=1
                                        ).then_inc(after, 1)
            for i in range(ROW_BUFS):
                pool.wait_ge(idx_in[i], 16)
                if i == 2:
                    pool.wait_ge(low_cut, PICKS)
                    pool.wait_ge(high_cut, PICKS)
                    pool.wait_ge(w1_lo_ready, 2)
                gather_tile(i)
            with pool.Fori(1, TILES // ROW_BUFS) as g:
                for i in range(ROW_BUFS):
                    pool.wait_ge(idx_in[i], (g + 1) * 16)
                    pool.wait_ge(feat_done, g * (ROW_BUFS * FEAT_BATCHES) + (i + 1 - ROW_BUFS) * FEAT_BATCHES)
                    pool.sem_inc(pool_passed, 1)
                    gather_tile(i)

        @block.tensor
        def _(pe):
            def feat_batch(g, buf, b):
                if b == 0:
                    pe.wait_ge(dense_in[buf], (g + 1) * 16)
                    pe.wait_ge(rows_in[buf], (g + 1) * (16 * len(GATHERED)))
                n = buf * FEAT_BATCHES + b
                pe.wait_ge(feat_out[b % 2], g * (ROW_BUFS * FEAT_BATCHES // 2) + n // 2 + 1)
                for s in range(b * TB, min(b * TB + TB, len(SLOTS))):
                    mm = pe.transpose(feat_ps[b % 2][:, s % TB, :], rows[:, buf, s, :], ident[:, :])
                mm.then_inc(feat_done, 1)

            def dot_tile(g, duo, i, between):
                buf = 2 * duo + i
                pe.wait_ge(feat_out[0], g * (ROW_BUFS * FEAT_BATCHES // 2) + (buf + 1) * (FEAT_BATCHES // 2) + 1)
                pe.wait_ge(feat_out[1], g * (ROW_BUFS * FEAT_BATCHES // 2) + (buf + 1) * (FEAT_BATCHES // 2) + 1)
                pe.wait_ge(pick_out, g * (2 * SETS) + (duo + 1) * SETS + 1)
                for k in range(DOT_BANKS):
                    pe.wait_ge(dot_out, g * (ROW_BUFS * DOT_BANKS) + buf * DOT_BANKS + k + 1)
                    for n in range(QB):
                        x = feats[:, i, (k * QB + n) * LANES:(k * QB + n + 1) * LANES, :]
                        mm = pe.matmul(dot_ps[k % 2][0:STAT, n, 0:LANES * LEFT], x.rearrange("d s f -> d (s f)")[:, 1:1 + STAT],
                                       x[:, :, 0:LEFT], start=True, stop=True)
                    mm.then_inc(dot_done, 1)
                    between(k)

            def spread_ids(u, before, k):
                pe.wait_ge(onehot_ready, before + k + 1)
                pe.sem_inc(pe_passed, 1)
                for t in range(2):
                    cols = slice(u * COLS, (u + 1) * COLS) if isinstance(u, int) else bass.ds(u * COLS, COLS)
                    mm = pe.matmul(ids_ps[:, t * COLS:(t + 1) * COLS], spread[:, 2 * k + t, :], ids_t[:, cols],
                                   start=True, stop=True)
                mm.then_inc(spread_done, 1)

            def pick(duo, before, k, pieces=range(PICK_PIECES)):
                for piece in pieces:
                    if piece == 0:
                        pe.wait_ge(onehot_ready, before + k + 2)
                        pe.wait_ge(pick_out, before + k + 1)
                    t, part_of = piece // (PICK_PIECES // 2), piece % (PICK_PIECES // 2)
                    for c in range(part_of * 2 * PICK_CHUNKS // PICK_PIECES, (part_of + 1) * 2 * PICK_CHUNKS // PICK_PIECES):
                        for part in range(PARTS):
                            mm = pe.matmul(pick_ps[:, t, :], parts[:, 2 * k + t, part, c, :],
                                           onehot[:, (duo * SETS + k) % 2, c, t * COLS:(t + 1) * COLS],
                                           start=(c == 0 and part == 0), stop=(c == PICK_CHUNKS - 1 and part == PARTS - 1))
                    if piece == PICK_PIECES - 1:
                        mm.then_inc(pick_done, 1)

            def tail_free(g, duo, m):
                if TURN_BATCHES <= m - 2 < L1_STEP:
                    pe.wait_ge(pairs_lo_ready, (g * 2 + duo) * PCHUNKS + m - 2 - TURN_BATCHES + 1)
                else:
                    pe.wait_ge(tail_out[m % 2], (g * 2 + duo) * emptied(TAIL_STEPS, m % 2) + emptied(m, m % 2) + 1)

            def tail_whole(g, duo, steps):
                for parity in range(2):
                    pe.wait_ge(tail_out[parity], (g * 2 + duo) * emptied(TAIL_STEPS, parity) + emptied(steps, parity) + 1)

            def turn(g, duo, m, ahead):
                if m == 0:
                    pe.wait_ge(dot_out, g * (ROW_BUFS * DOT_BANKS) + 2 * (duo + 1) * DOT_BANKS + 2)
                if ahead or m not in SPARED:
                    tail_free(g, duo, m)
                for h in range(m * TB, min(m * TB + TB, LEFT // 2)):
                    mm = pe.transpose(tail_bank(m, ahead)[:, h % TB, 0:STAT], dots[0:STAT, 2 * h:2 * h + 2, :], ident[0:STAT, 0:STAT])
                mm.then_inc(tail_done, 1)

            def turn_back(g, duo, c, ahead):
                tail_whole(g, duo, turned_for(c))
                m = TURN_BATCHES + c
                if ahead:
                    tail_free(g, duo, m)
                pe.sem_inc(pe_passed, 1)
                to = tail_bank(m, ahead)[0:PK, :, :].rearrange("p t s -> p (t s)")
                for j in range(LANES):
                    mm = pe.transpose(to[:, j * QD:(j + 1) * QD], pairs[:, j, c * PK:(c + 1) * PK], ident[0:QD, 0:QD])
                mm.then_inc(tail_done, 1)

            def layer1_dense(g, duo, n, ahead):
                m = L1_STEP + n
                if ahead:
                    tail_free(g, duo, m)
                pe.matmul(tail_bank(m, ahead)[:, 0:2, :], w1_dense[:, n * P:(n + 1) * P],
                          dense_t[:, duo, :, :, :].rearrange("d j i q -> d (j i q)"), start=True, stop=False)

            def layer1_pairs(g, duo, n, c, ahead):
                for weights, values in ((w1_hi, pairs_hi), (w1_hi, pairs_lo), (w1_lo, pairs_hi)):
                    mm = pe.matmul(tail_bank(L1_STEP + n, ahead)[:, 0:2, :], weights[:, c, n * P:(n + 1) * P], values[:, c, :],
                                   start=False, stop=(c == PCHUNKS - 1 and weights is w1_lo))
                if c == PCHUNKS - 1:
                    mm.then_inc(tail_done, 1)

            def pairs_ready(g, duo, c):
                pe.wait_ge(pairs_lo_ready, (g * 2 + duo) * PCHUNKS + c + 1)
                pe.wait_ge(pairs_hi_ready, (g * 2 + duo) * PCHUNKS + c + 1)
                pe.sem_inc(pe_passed, 1)

            def layer1(g, duo, ahead):
                if ahead:
                    for n in range(H1 // P):
                        layer1_dense(g, duo, n, ahead)
                        for c in range(PCHUNKS):
                            if n == 0:
                                pairs_ready(g, duo, c)
                            layer1_pairs(g, duo, n, c, ahead)
                else:
                    for c in range(PCHUNKS):
                        pairs_ready(g, duo, c)
                        for n in range(H1 // P):
                            layer1_pairs(g, duo, n, c, ahead)

            def layer2(g, duo):
                for n in range(H2 // P):
                    m = L2_STEP + n
                    tail_free(g, duo, m)
                    for c in range(H1 // P):
                        if n == 0:
                            tail_whole(g, duo, L1_STEP + c + 1)
                        mm = pe.matmul(tail_ps[m % 2][:, 0:2, :], w2[:, c, n * P:(n + 1) * P], h1[:, c, :],
                                       start=(c == 0), stop=(c == H1 // P - 1))
                    mm.then_inc(tail_done, 1)

            def layer3(g, duo):
                for c in range(H2 // P):
                    tail_whole(g, duo, L2_STEP + c + 1)
                    mm = pe.matmul(tail_ps[L3_STEP % 2][0:1, 0:2, :], w3[:, c:c + 1], h2[:, c, :],
                                   start=(c == 0), stop=(c == H2 // P - 1))
                mm.then_inc(tail_done, 1)

            def first_half(g, duo, ahead, alone=False):
                def turn_features(k):
                    for b in range(FEAT_BATCHES):
                        if FEATS_AFTER[b] == k:
                            feat_batch(g, 2 * duo + 1, b)

                if ahead:
                    spread_ids(2 * g + duo + 1, g * (2 * SETS) + (duo + 1) * SETS, 0)
                dot_tile(g, duo, 0, lambda k: turn_features(k) if not alone else None)
                if alone:
                    for k in sorted(set(FEATS_AFTER)):
                        turn_features(k)

            def second_half(g, duo, ahead):
                other, before = 1 - duo, g * (2 * SETS) + (duo + 1) * SETS

                def picks(k, *pieces):
                    if ahead:
                        pick(other, before, k, pieces)

                def spread(k):
                    if ahead:
                        spread_ids(2 * g + duo + 1, before, k)

                def next_features(*batches):
                    for b in batches:
                        if ahead:
                            feat_batch(g + duo, 2 * other, b)

                picks(0, 0)
                dot_tile(g, duo, 1, lambda k: spread(1) if k == 1 else picks(0, k // 2) if k in (2, 4, 6) else None)
                picks(0, 4, 5)
                if not ahead:
                    layer1_dense(g, duo, 2, ahead)
                    layer1_dense(g, duo, 3, ahead)
                turn(g, duo, 0, ahead)
                turn(g, duo, 1, ahead)
                picks(0, 6, 7)
                spread(2)
                turn(g, duo, 2, ahead)
                turn(g, duo, 3, ahead)
                picks(1, 0, 1, 2, 3)
                if not ahead:
                    layer1_dense(g, duo, 0, ahead)
                    layer1_dense(g, duo, 1, ahead)
                turn_back(g, duo, 0, ahead)
                turn_back(g, duo, 1, ahead)
                picks(1, 4, 5, 6)
                turn_back(g, duo, 2, ahead)
                picks(1, 7)
                layer1(g, duo, ahead)
                picks(2, 0, 1)
                next_features(0, 1)
                layer2(g, duo)
                next_features(2)
                picks(2, 2, 3)
                next_features(3, 4)
                picks(2, 4, 5)
                next_features(5)
                picks(2, 6, 7)
                layer3(g, duo)

            def spread_for_act(k):
                to = tail_ps[k % 2].rearrange("p t s -> p (t s)")
                for t in range(2):
                    mm = pe.matmul(to[:, t * COLS:(t + 1) * COLS], spread[:, 2 * k + t, :], ids_t[:, 0:COLS], start=True, stop=True)
                mm.then_inc(act_spread_done, 1)

            pe.sem_inc(pick_done, 2)
            pe.wait_ge(ident_ready, 1)
            pe.wait_ge(ids_hl_ready, 2)
            for m in range(TILES // TB):
                if m >= 2:
                    pe.wait_ge(ids_t_ready, m - 1)
                for t in range(TB):
                    mm = pe.transpose(tail_ps[m % 2][0:2 * PICKS, t, :], ids_hl[:, m * TB + t, :], ident[:, :])
                mm.then_inc(ids_turned, 1)
            pe.wait_ge(ids_t_ready, TILES // TB)
            pe.wait_ge(spread_ready, 1)
            spread_ids(0, 0, 0)
            spread_for_act(0)
            spread_for_act(1)
            for k in range(SETS):
                if k + 1 < SETS:
                    spread_ids(0, 0, k + 1)
                pe.wait_ge(act_onehot_ready, (k + 1) * ACT_CHUNKS)
                if k + 2 < SETS:
                    spread_for_act(k + 2)
                pe.wait_ge(high_cut, 2 * (k + 1))
                pe.wait_ge(low_cut, 2 * (k + 1))
                pick(0, 0, k)
                for b in (2 * k, 2 * k + 1):
                    feat_batch(0, 0, b)
            pe.wait_ge(w1_summed, 1)
            pe.wait_ge(w1_hi_ready, PCHUNKS)
            pe.wait_ge(w1_lo_ready, PCHUNKS)
            pe.wait_ge(w2_in, 16)
            pe.wait_ge(small_in, 48)
            pe.wait_ge(feats_zero, 2)
            first_half(0, 0, True, alone=True)
            with pe.Fori(0, GROUPS - 1) as g:
                second_half(g, 0, True)
                first_half(g, 1, True)
                second_half(g, 1, True)
                first_half(g + 1, 0, True)
            second_half(GROUPS - 1, 0, True)
            first_half(GROUPS - 1, 1, False)
            second_half(GROUPS - 1, 1, False)

        def feat_views(i, b):
            features = SLOTS[b * TB:b * TB + TB]
            for at, f, n in runs(features):
                yield feats[:, i, :, f:f + n].rearrange("d s f -> d f s"), feat_ps[b % 2][:, at:at + n, :]

        def dot_views(i, k, j):
            at, low = i * QT + k * QB, FEATS_PAD * j
            return (dots[low:low + LEFT, :, at:at + QB],
                    dot_ps[k % 2][low:low + LEFT, :, j * LEFT:(j + 1) * LEFT].rearrange("a n b -> a b n"))

        def turn_views(m, ahead):
            for b in range(2 * m * TB, min(2 * m * TB + 2 * TB, LEFT)):
                low = QD * (b % 2)
                src = tail_bank(m, ahead)[low:low + QD, (b // 2) % TB, :].rearrange("p (j a) -> p j a", j=LANES)
                yield pairs[:, :, pair_base(b):pair_base(b) + LEFT - b], src[:, :, b:LEFT]

        def layer_views(m, ahead):
            src = tail_bank(m, ahead)[:, 0:2, :].rearrange("p t s -> p (t s)")
            if m < L2_STEP:
                n = m - L1_STEP
                return h1[:, n, :], src, bias1[:, n:n + 1]
            n = m - L2_STEP
            return h2[:, n, :], src, bias2[:, n:n + 1]

        @block.vector
        def _(dve):
            def features(g, buf, b):
                dve.wait_ge(feat_done, g * (ROW_BUFS * FEAT_BATCHES) + buf * FEAT_BATCHES + b + 1)
                i = buf % 2
                if b == 0:
                    nc.vector.tensor_copy(dense_t[:, buf // 2, :, i, :], feat_ps[0][:, 0, :].rearrange("d (q j) -> d j q", j=LANES))
                for to, src in feat_views(i, b):
                    last = nc.vector.tensor_copy(to, src)
                last.then_inc(feat_out[0], 1)

            def build_onehot(duo, before, k, chunks, final=PICK_CHUNKS - 1):
                for c in chunks:
                    if c == 0:
                        dve.wait_ge(spread_done, before + k + 1)
                        dve.wait_ge(pick_done, before + k + 1)
                    last = nc.vector.tensor_scalar(onehot[:, (duo * SETS + k) % 2, c, :], ids_ps[0:PICK_K, :],
                                                   row_of[0:PICK_K, c:c + 1], None, ALU.is_equal)
                    if c == final:
                        last.then_inc(onehot_ready, 1)

            def tail(g, duo, m, ahead):
                dve.wait_ge(tail_done, g * (2 * TAIL_STEPS) + duo * TAIL_STEPS + m + 1)
                if m < TURN_BATCHES:
                    for to, src in turn_views(m, ahead):
                        last = nc.vector.tensor_copy(to, src)
                elif m < L1_STEP:
                    c = m - TURN_BATCHES
                    n = (g * 2 + duo) * PCHUNKS + c
                    if c >= 2:
                        dve.wait_ge(pairs_hi_ready, n - 1)
                        dve.sem_inc(dve_passed, 1)
                    masked, src = pairs_masked[:, c % 2, :], tail_bank(m, ahead)[0:PK, 0:2, :].rearrange("p t s -> p (t s)")
                    nc.vector.tensor_scalar(masked.bitcast(I32), src.bitcast(I32), HIGH_BITS, None, ALU.bitwise_and
                                            ).then_inc(pairs_mask_ready, 1)
                    dve.wait_ge(pairs_mask_ready, n + 1)
                    nc.vector.tensor_tensor(pairs_lo[:, c, :], src, masked, ALU.subtract).then_inc(pairs_lo_ready, 1)
                    return
                elif m < L3_STEP:
                    to, src, bias = layer_views(m, ahead)
                    last = nc.vector.tensor_scalar(to, src, bias, 0.0, ALU.add, ALU.max)
                else:
                    u = g * 2 + duo
                    to = y_v[:, u, :, :, :] if isinstance(u, int) else \
                        y_v[:, bass.ds(u, 1), :, :, :].rearrange("o u j i q -> o (u j) i q")
                    src = tail_ps[m % 2][0:1, 0:2, :].rearrange("o t s -> o (t s)")
                    last = nc.vector.tensor_copy(to, src.rearrange("o (j i q) -> o j i q", j=LANES, i=2))
                last.then_inc(tail_out[1], 1)

            def first_half(g, duo, ahead, alone=False):
                before = g * (2 * SETS) + (duo + 1) * SETS
                if alone:
                    build_onehot(1 - duo, before, 0, range(PICK_CHUNKS))
                for b in range(0, FEAT_BATCHES, 2):
                    if ahead and not alone:
                        build_onehot(1 - duo, before, 0, (range(4), range(4, 6), range(6, 8))[b // 2])
                    features(g, 2 * duo + 1, b)

            def second_half(g, duo, ahead):
                other, before = 1 - duo, g * (2 * SETS) + (duo + 1) * SETS
                if ahead:
                    build_onehot(other, before, 1, range(PICK_CHUNKS))
                for m in sorted({*range(1, TAIL_STEPS, 2), *range(TURN_BATCHES, L1_STEP)}):
                    tail(g, duo, m, ahead)
                    if ahead:
                        if m == L2_STEP - 2:
                            features(g + duo, 2 * other, 0)
                        if m == L2_STEP:
                            features(g + duo, 2 * other, 2)
                            features(g + duo, 2 * other, 4)
                    if ahead and m in BUILD_AFTER:
                        piece = BUILD_AFTER.index(m)
                        build_onehot(other, before, 2, range(piece * BUILD_PIECE, (piece + 1) * BUILD_PIECE))
            for s in (feat_out[0], tail_out[1], onehot_ready):
                dve.sem_inc(s, 1)
            nc.vector.memset(feats[:, 0, :, FEATS:FEATS_PAD], 0.0).then_inc(feats_zero, 1)
            dve.wait_ge(row_int_ready, 1)
            nc.vector.tensor_copy(row_of[:, :], row_int[:, :]).then_inc(row_of_ready, 1)
            nc.vector.tensor_scalar(minus_row[:, :], row_int[:, :], -1.0, None, ALU.mult).then_inc(minus_row_ready, 1)
            dve.wait_ge(ids_in, 16)
            for k, (f, _) in enumerate(PICK_SETS):
                last = nc.vector.tensor_copy(ids_hi[:, :, 2 * k:2 * k + 2], ids_all[:, :, f:f + 2])
            last.then_inc(ids_hi_ready, 1)
            dve.wait_ge(ids_hi_ready, 1)
            nc.vector.tensor_copy(ids_hl[:, :, 0:PICKS], ids_hi[:, :, :]).then_inc(ids_hl_ready, 1)
            for k, (f, _) in enumerate(PICK_SETS):
                last = nc.vector.tensor_tensor(ids_hl[:, :, PICKS + 2 * k:PICKS + 2 * k + 2], ids_all[:, :, f:f + 2],
                                               ids_hi[:, :, 2 * k:2 * k + 2], ALU.subtract)
            last.then_inc(ids_hl_ready, 1)
            for m in range(TILES // TB):
                dve.wait_ge(ids_turned, m + 1)
                nc.vector.tensor_copy(ids_t[:, m * TB * P:(m + 1) * TB * P],
                                      tail_ps[m % 2][0:2 * PICKS, :, :].rearrange("p t s -> p (t s)")).then_inc(ids_t_ready, 1)
            dve.wait_ge(row_of_ready, 1)

            def cut(*numbers):
                for n in numbers:
                    dve.wait_ge(table_in[n], 16)
                    if n >= 2:
                        dve.wait_ge(high_cut, n - 1)
                        dve.wait_ge(low_cut, n - 1)
                    nc.vector.tensor_scalar(high[n % 2].bitcast(I32), stage[n].bitcast(I32), HIGH_BITS, None,
                                            ALU.bitwise_and).then_inc(high_ready, 1)
                for n in numbers:
                    dve.wait_ge(high_ready, n + 1)
                    nc.vector.tensor_tensor(parts[:, n, 1, :, :], stage[n], high[n % 2], ALU.subtract).then_inc(low_cut, 1)

            build_onehot(0, 0, 0, range(DVE_CHUNKS), DVE_CHUNKS - 1)
            cut(0, 1)
            build_onehot(0, 0, 1, range(DVE_CHUNKS), DVE_CHUNKS - 1)
            cut(2, 3)
            dve.wait_ge(low_cut, 4)
            nc.vector.memset(feats[:, 1, :, FEATS:FEATS_PAD], 0.0).then_inc(feats_zero, 1)
            cut(4, 5)
            build_onehot(0, 0, 2, range(DVE_CHUNKS), DVE_CHUNKS - 1)
            features(0, 0, 0)
            features(0, 0, 2)
            dve.wait_ge(w1p_in, 48)
            dve.wait_ge(act_onehot_ready, SETS * ACT_CHUNKS)
            for c in range(PCHUNKS):
                if c >= 2:
                    dve.wait_ge(w1_hi_ready, c - 1)
                    dve.wait_ge(w1_lo_ready, c - 1)
                nc.vector.tensor_scalar(apart[c % 2][0:PK, :].bitcast(I32), w1_stage[c].bitcast(I32), HIGH_BITS, None,
                                        ALU.bitwise_and).then_inc(w1_masked, 1)
                dve.wait_ge(w1_masked, c + 1)
                nc.vector.tensor_tensor(w1_lo[:, c, :], w1_stage[c], apart[c % 2][0:PK, :], ALU.subtract).then_inc(w1_lo_ready, 1)
            features(0, 0, 4)
            dve.wait_ge(w1_in, 32)
            nc.vector.tensor_tensor(w1_dense[:, :], w1_dense[:, :], w1_dense2, ALU.add).then_inc(w1_summed, 1)
            first_half(0, 0, True, alone=True)
            with dve.Fori(0, GROUPS - 1) as g:
                second_half(g, 0, True)
                first_half(g, 1, True)
                second_half(g, 1, True)
                first_half(g + 1, 0, True)
            second_half(GROUPS - 1, 0, True)
            first_half(GROUPS - 1, 1, False)
            second_half(GROUPS - 1, 1, False)

        @block.scalar
        def _(act):
            def features(g, buf, b):
                act.wait_ge(feat_done, g * (ROW_BUFS * FEAT_BATCHES) + buf * FEAT_BATCHES + b + 1)
                for to, src in feat_views(buf % 2, b):
                    last = nc.scalar.copy(to, src)
                last.then_inc(feat_out[1], 1)

            def tile_dots(g, duo, i, with_features=False):
                for k in range(DOT_BANKS):
                    act.wait_ge(dot_done, g * (ROW_BUFS * DOT_BANKS) + (2 * duo + i) * DOT_BANKS + k + 1)
                    for j in range(LANES):
                        last = nc.scalar.copy(*dot_views(i, k, j))
                    last.then_inc(dot_out, 1)
                    for b in range(1, FEAT_BATCHES, 2):
                        if with_features and FEATS_AFTER[b] == k:
                            features(g, 2 * duo + 1, b)

            def picked(before, k):
                act.wait_ge(pick_done, before + k + 3)
                f = 1 + PICK_SETS[k][0]
                nc.scalar.copy(feats[:, :, :, f:f + 2].rearrange("d i s f -> d f i s"),
                               pick_ps[:, :, :].rearrange("d f (i s) -> d f i s", i=2)).then_inc(pick_out, 1)

            def tail(g, duo, ahead, *steps):
                for m in steps:
                    act.wait_ge(tail_done, g * (2 * TAIL_STEPS) + duo * TAIL_STEPS + m + 1)
                    if m < TURN_BATCHES:
                        for to, src in turn_views(m, ahead):
                            last = nc.scalar.copy(to, src)
                    else:
                        to, src, bias = layer_views(m, ahead)
                        last = nc.scalar.activation(to, src, ACT.Relu, bias=bias)
                    last.then_inc(tail_out[0], 1)

            def take_pairs(g, duo):
                for c in range(PCHUNKS):
                    act.wait_ge(pairs_mask_ready, (g * 2 + duo) * PCHUNKS + c + 1)
                    nc.scalar.copy(pairs_hi[:, c, :], pairs_masked[:, c % 2, :]).then_inc(pairs_hi_ready, 1)

            def first_half(g, duo, ahead, alone=False):
                tile_dots(g, duo, 0, with_features=not alone)
                for b in range(1, FEAT_BATCHES, 2):
                    if alone:
                        features(g, 2 * duo + 1, b)

            def second_half(g, duo, ahead):
                def ready(k):
                    if ahead:
                        picked(g * (2 * SETS) + (duo + 1) * SETS, k)

                def next_features(b):
                    if ahead:
                        features(g + duo, 2 * (1 - duo), b)

                tile_dots(g, duo, 1)
                tail(g, duo, ahead, 0)
                ready(0)
                tail(g, duo, ahead, 2)
                take_pairs(g, duo)
                ready(1)
                tail(g, duo, ahead, 8, 10)
                next_features(1)
                tail(g, duo, ahead, 12)
                next_features(3)
                next_features(5)
                ready(2)

            act.dma_start(w1_dense[:, :], W1[0:DIM, :]).then_inc(w1_in, 16)
            act.dma_start(w1_dense2, W1[DIM + PAIRS:, :]).then_inc(w1_in, 16)
            with nc.allow_non_contiguous_dma(reason="1024 words of biases and of the last layer"):
                act.dma_start(bias1[:, :], b1.rearrange("(c p) -> p c", p=P)).then_inc(small_in, 16)
                act.dma_start(bias2[:, :], b2.rearrange("(c p) -> p c", p=P)).then_inc(small_in, 16)
                act.dma_start(w3[:, :], W3.rearrange("(c p) one -> p (c one)", p=P)).then_inc(small_in, 16)
            for s, n in ((feat_out[1], 1), (dot_out, 2), (tail_out[0], 1), (pick_out, 1)):
                act.sem_inc(s, n)
            act.wait_ge(minus_row_ready, 1)

            def build_onehot(k):
                act.wait_ge(act_spread_done, k + 1)
                if k >= 2:
                    act.wait_ge(pick_done, k + 1)
                for c in range(DVE_CHUNKS, PICK_CHUNKS, 2):
                    for e in (c, c + 1):
                        n = k * ACT_CHUNKS + e - DVE_CHUNKS
                        if n >= 2:
                            act.wait_ge(act_onehot_ready, n - 1)
                        nc.scalar.activation(apart[e % 2], tail_ps[k % 2][0:PICK_K, :, :].rearrange("k t s -> k (t s)"), ACT.Square,
                                             bias=minus_row[0:PICK_K, e:e + 1]).then_inc(apart_ready, 1)
                    for e in (c, c + 1):
                        act.wait_ge(apart_ready, k * ACT_CHUNKS + e - DVE_CHUNKS + 1)
                        nc.scalar.activation(onehot[:, k % 2, e, :], apart[e % 2], ACT.Relu, bias=1.0, scale=-1.0
                                             ).then_inc(act_onehot_ready, 1)

            def take_high(*numbers):
                for n in numbers:
                    act.wait_ge(high_ready, n + 1)
                    nc.scalar.copy(parts[:, n, 0, :, :], high[n % 2]).then_inc(high_cut, 1)

            build_onehot(0)
            take_high(0, 1)
            build_onehot(1)
            take_high(2, 3, 4, 5)
            act.wait_ge(feats_zero, 2)
            picked(0, 0)
            build_onehot(2)
            features(0, 0, 1)
            picked(0, 1)
            features(0, 0, 3)
            for c in range(PCHUNKS):
                act.wait_ge(w1_masked, c + 1)
                nc.scalar.copy(w1_hi[:, c, :], apart[c % 2][0:PK, :]).then_inc(w1_hi_ready, 1)
            picked(0, 2)
            features(0, 0, 5)
            first_half(0, 0, True, alone=True)
            with act.Fori(0, GROUPS - 1) as g:
                second_half(g, 0, True)
                first_half(g, 1, True)
                second_half(g, 1, True)
                first_half(g + 1, 0, True)
            second_half(GROUPS - 1, 0, True)
            first_half(GROUPS - 1, 1, False)
            second_half(GROUPS - 1, 1, False)


_TABLE_NAMES = [f"tbl_{f}" for f in range(TABLES)]


def kernel(**inputs):
    import numpy as _np
    import concourse.bacc as _bacc
    from concourse.bass_utils import run_bass_kernel_spmd as _run

    nc = _bacc.Bacc("TRN2", target_bir_lowering=False, num_devices=1)
    arrays, d = {}, {}
    for name in ["r_dense_features", "ids", *_TABLE_NAMES, "W_top1", "b_top1", "W_top2", "b_top2", "W_top3"]:
        a = _np.ascontiguousarray(inputs[name])
        arrays["in_" + name] = a
        d[name] = nc.dram_tensor("in_" + name, a.shape, mybir.dt.from_np(a.dtype), kind="ExternalInput").ap()
    out = nc.dram_tensor("out_y", (BATCH, 1), F32, kind="ExternalOutput").ap()
    build(nc, d["r_dense_features"], d["ids"], [d[t] for t in _TABLE_NAMES], d["W_top1"], d["b_top1"], d["W_top2"],
          d["b_top2"], d["W_top3"], out)
    return _run(nc, [arrays], core_ids=[0]).results[0]["out_y"]
```
